# Optimizing a Trainium2 kernel written in Bass

```python
import numpy as np
import jax
import jax.numpy as jnp

def _softmax(x, axis=-1):
    return jax.nn.softmax(x, axis=axis)

def _gelu(x):
    return jax.nn.gelu(x, approximate=True)

def _silu(x):
    return jax.nn.silu(x)

def _sigmoid(x):
    return jax.nn.sigmoid(x)

def _layernorm(x, axis=-1, eps=1e-05):
    m = jnp.mean(x, axis=axis, keepdims=True)
    v = jnp.var(x, axis=axis, keepdims=True)
    return (x - m) / jnp.sqrt(v + eps)

def _scatter_add(tgt, idx, src, axis=0):
    return tgt.at[idx].add(src)

def _segment_sum(src, seg, n):
    return jax.ops.segment_sum(src, seg, n)
kernel_name = 'mk_gnn_ffn_d2_gnn_r8_eb111d'

def setup_inputs(seed: int=0):
    np.random.seed(seed)
    _w = jnp.asarray

    def _rec_inputs():
        import jax
        import jax.numpy as jnp
        _gk = jax.random.key(seed)
        x = -0.0002928 + 1 * jax.random.normal(jax.random.fold_in(_gk, 1), (1024, 512), jnp.float32)
        _s = jax.random.randint(jax.random.fold_in(_gk, 2), (8192,), 0, 1024, jnp.int32)
        _d = jax.random.randint(jax.random.fold_in(_gk, 3), (8192,), 0, 1024, jnp.int32)
        _loop = jnp.arange(1024, dtype=jnp.int32)
        src = jnp.concatenate([_s, _d, _loop])
        dst = jnp.concatenate([_d, _s, _loop])
        _o = jnp.argsort(dst, stable=True)
        src = src[_o]
        dst = dst[_o]
        return (x, src, dst)
    x, src, dst = _rec_inputs()

    def _L0_gnn_setup():
        import jax, jax.numpy as jnp
        import numpy as np
        N_NODES = 1024
        N_EDGES = 32768
        D_IN = 512
        D_OUT = 512
        key = jax.random.key(seed)
        k1, k2, k3 = jax.random.split(key, 3)
        x = jax.random.normal(k1, (N_NODES, D_IN), dtype=jnp.float32)
        edge_index = jax.random.randint(k2, (2, N_EDGES), 0, N_NODES, dtype=jnp.int64)
        weight = jax.random.normal(k3, (D_IN, D_OUT), dtype=jnp.float32)
        bias = jnp.zeros((D_OUT,), dtype=jnp.float32)
        return {'x': x, 'edge_index': edge_index, 'weight': weight, 'bias': bias}
    _L0_gnn_all = _L0_gnn_setup()
    _L0_gnn_in = {k: v for k, v in _L0_gnn_all.items() if k in ('weight', 'bias')}
    del _L0_gnn_all

    def _L0_ffn_setup():
        import jax, jax.numpy as jnp
        import numpy as np
        B, S, D, F, E, TOP_K = (8, 512, 512, 1024, 16, 2)
        LN_EPS = 1e-05
        key = jax.random.key(seed)
        ks = jax.random.split(key, 5)
        s = 0.02
        x = jax.random.normal(ks[0], (B, S, D), dtype=jnp.float32)
        gate_w = jax.random.normal(ks[1], (D, E), dtype=jnp.float32) * s
        gate_b = jnp.zeros((E,), jnp.float32)
        w1 = jax.random.normal(ks[2], (E, D, F), dtype=jnp.float32) * s
        b1 = jnp.zeros((E, F), jnp.float32)
        w2 = jax.random.normal(ks[3], (E, F, D), dtype=jnp.float32) * s
        b2 = jnp.zeros((E, D), jnp.float32)
        gamma = jnp.ones((E, D), jnp.float32)
        beta = jnp.zeros((E, D), jnp.float32)
        return {'x': x, 'gate_w': gate_w, 'gate_b': gate_b, 'w1': w1, 'b1': b1, 'w2': w2, 'b2': b2, 'gamma': gamma, 'beta': beta}
    _L0_ffn_all = _L0_ffn_setup()
    _L0_ffn_in = {k: v for k, v in _L0_ffn_all.items() if k in ('gate_w', 'gate_b', 'w1', 'b1', 'w2', 'b2', 'gamma', 'beta')}
    del _L0_ffn_all

    def _L1_gnn_setup():
        import jax, jax.numpy as jnp
        import numpy as np
        N_NODES = 4096
        N_EDGES = 32768
        D = 512
        NUM_EXPERTS = 4
        TOP_K = 2
        LAYERS = 2
        key = jax.random.key(seed)
        ks = jax.random.split(key, 8)
        x = jax.random.normal(ks[0], (N_NODES, D), dtype=jnp.float32)
        edge_index = jax.random.randint(ks[1], (2, N_EDGES), 0, N_NODES, dtype=jnp.int64)
        s = 1.0 / np.sqrt(D)
        gate_W = jax.random.uniform(ks[2], (D, NUM_EXPERTS), jnp.float32, -s, s)
        gate_b = jax.random.uniform(ks[3], (NUM_EXPERTS,), jnp.float32, -s, s)
        Wl = jax.random.uniform(ks[4], (NUM_EXPERTS, LAYERS, D, D), jnp.float32, -s, s)
        bl = jax.random.uniform(ks[5], (NUM_EXPERTS, LAYERS, D), jnp.float32, -s, s)
        Wr = jax.random.uniform(ks[6], (NUM_EXPERTS, LAYERS, D, D), jnp.float32, -s, s)
        return {'x': x, 'gate_W': gate_W, 'gate_b': gate_b, 'Wl': Wl, 'bl': bl, 'Wr': Wr, 'edge_index': edge_index}
    _L1_gnn_all = _L1_gnn_setup()
    _L1_gnn_in = {k: v for k, v in _L1_gnn_all.items() if k in ('gate_W', 'gate_b', 'Wl', 'bl', 'Wr')}
    del _L1_gnn_all

    def _L1_ffn_setup():
        import jax, jax.numpy as jnp
        import numpy as np
        NEXPERTS = 16
        key = jax.random.key(seed)
        k1, k2, k3, k4 = jax.random.split(key, 4)
        B, S, D = (4, 256, 512)
        E, Sets, F = (16, 4, 32)
        scale = 0.02
        return {'x': jax.random.normal(k1, (B, S, D), dtype=jnp.float32), 'controller': jax.random.normal(k2, (D, E, Sets), dtype=jnp.float32) * scale, 'f1': jax.random.normal(k3, (D, E, Sets, F), dtype=jnp.float32) * scale, 'f2': jax.random.normal(k4, (E, Sets, F, D), dtype=jnp.float32) * scale}
    _L1_ffn_all = _L1_ffn_setup()
    _L1_ffn_in = {k: v for k, v in _L1_ffn_all.items() if k in ('controller', 'f1', 'f2')}
    del _L1_ffn_all
    return {'x': x, 'src': src, 'dst': dst, 'L0_gnn_weight': _L0_gnn_in['weight'], 'L0_gnn_bias': _L0_gnn_in['bias'], 'L0_ffn_gate_w': _L0_ffn_in['gate_w'], 'L0_ffn_gate_b': _L0_ffn_in['gate_b'], 'L0_ffn_w1': _L0_ffn_in['w1'], 'L0_ffn_b1': _L0_ffn_in['b1'], 'L0_ffn_w2': _L0_ffn_in['w2'], 'L0_ffn_b2': _L0_ffn_in['b2'], 'L0_ffn_gamma': _L0_ffn_in['gamma'], 'L0_ffn_beta': _L0_ffn_in['beta'], 'L1_gnn_gate_W': _L1_gnn_in['gate_W'], 'L1_gnn_gate_b': _L1_gnn_in['gate_b'], 'L1_gnn_Wl': _L1_gnn_in['Wl'], 'L1_gnn_bl': _L1_gnn_in['bl'], 'L1_gnn_Wr': _L1_gnn_in['Wr'], 'L1_ffn_controller': _L1_ffn_in['controller'], 'L1_ffn_f1': _L1_ffn_in['f1'], 'L1_ffn_f2': _L1_ffn_in['f2']}

def reference(x, src, dst, L0_gnn_weight, L0_gnn_bias, L0_ffn_gate_w, L0_ffn_gate_b, L0_ffn_w1, L0_ffn_b1, L0_ffn_w2, L0_ffn_b2, L0_ffn_gamma, L0_ffn_beta, L1_gnn_gate_W, L1_gnn_gate_b, L1_gnn_Wl, L1_gnn_bl, L1_gnn_Wr, L1_ffn_controller, L1_ffn_f1, L1_ffn_f2):
    import jax
    import jax.numpy as jnp

    def _L0_gnn_ref(x, edge_index, weight, bias):
        import jax, jax.numpy as jnp
        import numpy as np
        N_NODES = 1024
        N_EDGES = 32768
        D_IN = 512
        D_OUT = 512
        n = x.shape[0]
        adj = jnp.zeros((n, n), dtype=x.dtype)
        adj = adj.at[edge_index[0], edge_index[1]].set(1.0)
        adj = adj.at[edge_index[1], edge_index[0]].set(1.0)
        adj = adj + jnp.eye(n, dtype=x.dtype)
        deg = jnp.sum(adj, axis=1)
        dinv = 1.0 / jnp.sqrt(deg)
        adj = adj * dinv[:, None] * dinv[None, :]
        return adj @ (x @ weight) + bias

    def _L0_ffn_ref(x, gate_w, gate_b, w1, b1, w2, b2, gamma, beta):
        import jax, jax.numpy as jnp
        import numpy as np
        B, S, D, F, E, TOP_K = (8, 512, 512, 1024, 16, 2)
        LN_EPS = 1e-05
        b, s, d = x.shape
        e = gate_w.shape[1]
        xf = x.reshape(-1, d)
        scores = xf @ gate_w + gate_b
        topk_s, topk_i = jax.lax.top_k(scores, TOP_K)
        topk_w = jax.nn.softmax(topk_s, axis=1)
        comb = (jax.nn.one_hot(topk_i, e, dtype=xf.dtype) * topk_w[..., None]).sum(1)
        out = jnp.zeros_like(xf)
        for eid in range(e):
            h = jax.nn.gelu(xf @ w1[eid] + b1[eid], approximate=False)
            y = h @ w2[eid] + b2[eid]
            mu = y.mean(axis=-1, keepdims=True)
            var = ((y - mu) ** 2).mean(axis=-1, keepdims=True)
            y = (y - mu) / jnp.sqrt(var + LN_EPS) * gamma[eid] + beta[eid]
            out = out + comb[:, eid:eid + 1] * y
        return out.reshape(b, s, d)

    def _L1_gnn_ref(x, gate_W, gate_b, Wl, bl, Wr, edge_index):
        import jax, jax.numpy as jnp
        import numpy as np
        N_NODES = 4096
        N_EDGES = 32768
        D = 512
        NUM_EXPERTS = 4
        TOP_K = 2
        LAYERS = 2
        n = x.shape[0]
        src, dst = (edge_index[0], edge_index[1])
        gates = jax.nn.softmax(x @ gate_W + gate_b, axis=-1)
        top_v, top_i = jax.lax.top_k(gates, TOP_K)
        deg = jax.ops.segment_sum(jnp.ones((src.shape[0],), x.dtype), dst, num_segments=n)
        inv_deg = jnp.where(deg > 0, 1.0 / jnp.maximum(deg, 1.0), 0.0)[:, None]

        def sage_conv(h, W_l, b_l, W_r):
            aggr = jax.ops.segment_sum(h[src], dst, num_segments=n) * inv_deg
            return aggr @ W_l + b_l + h @ W_r
        expert_outs = []
        for e in range(NUM_EXPERTS):
            h = x
            for l in range(LAYERS):
                h = sage_conv(h, Wl[e, l], bl[e, l], Wr[e, l])
                h = jax.nn.relu(h)
            expert_outs.append(h)
        expert_outputs = jnp.stack(expert_outs, axis=1)
        sel = jnp.take_along_axis(expert_outputs, top_i[:, :, None], axis=1)
        out = jnp.sum(sel * top_v[:, :, None], axis=1)
        return out

    def _L1_ffn_ref(x, controller, f1, f2):
        import jax, jax.numpy as jnp
        import numpy as np
        NEXPERTS = 16
        B, S, D = x.shape
        t = NEXPERTS
        grouped = x.reshape(B, S // t, t, D)
        cont_logits = jnp.einsum('bgtd,des->bgtes', grouped, controller)
        tie = jnp.linspace(0.0, 1e-06, t, dtype=x.dtype).reshape(t, 1, 1)
        cont_logits = cont_logits + tie
        cont_perm = (cont_logits == jnp.max(cont_logits, axis=-3, keepdims=True)).astype(x.dtype)
        intermediate = jnp.einsum('bgtd,desf->bgtesf', grouped, f1)
        inner = jnp.einsum('bgtesf,bgtes->bgesf', intermediate, cont_perm)
        inner = jax.nn.relu(inner)
        inter2 = jnp.einsum('bgesf,esfd->bgesd', inner, f2)
        result = jnp.einsum('bgesd,bgtes->bgtd', inter2, cont_perm)
        return result.reshape(B, S, D)
    edge_index = jnp.stack([src, dst])
    x = x + _L0_gnn_ref(_layernorm(x, axis=-1), edge_index, L0_gnn_weight, L0_gnn_bias)
    x = x + _L0_ffn_ref(_layernorm(x, axis=-1)[None], L0_ffn_gate_w, L0_ffn_gate_b, L0_ffn_w1, L0_ffn_b1, L0_ffn_w2, L0_ffn_b2, L0_ffn_gamma, L0_ffn_beta)[0]
    x = x + _L1_gnn_ref(_layernorm(x, axis=-1), L1_gnn_gate_W, L1_gnn_gate_b, L1_gnn_Wl, L1_gnn_bl, L1_gnn_Wr, edge_index)
    x = x + _L1_ffn_ref(_layernorm(x, axis=-1)[None], L1_ffn_controller, L1_ffn_f1, L1_ffn_f2)[0]
    return x

_drawn_inputs = setup_inputs


def setup_inputs(seed=0):
    import zlib

    import numpy as np

    out = dict(_drawn_inputs(seed))
    spreads = {'L0_gnn_bias': (0.0, 0.313),
     'L0_ffn_gate_b': (0.0, 0.1),
     'L0_ffn_b1': (0.0, 0.326),
     'L0_ffn_b2': (0.0, 0.1),
     'L0_ffn_gamma': (1.0, 0.6),
     'L0_ffn_beta': (0.0, 0.636)}
    factors = {'L1_gnn_gate_W': 4.816,
     'L1_gnn_gate_b': 8.0,
     'L1_gnn_Wl': 5.572,
     'L1_gnn_bl': 8.0,
     'L1_gnn_Wr': 4.092,
     'L1_ffn_controller': 4.744,
     'L1_ffn_f1': 5.555,
     'L1_ffn_f2': 4.633}
    for name, (base, spread) in spreads.items():
        noise = np.random.default_rng([zlib.crc32(name.encode()), seed]).standard_normal(out[name].shape)
        drawn = base * np.exp(spread * noise) if base else spread * noise
        out[name] = jnp.asarray(drawn.astype(out[name].dtype))
    for name, factor in factors.items():
        out[name] = (out[name] * factor).astype(out[name].dtype)
    return out
```

```python
from contextlib import ExitStack

import concourse.bass as bass
import concourse.mybir as mybir

P = 128
ALU = mybir.AluOpType
ACT = mybir.ActivationFunctionType
AX = mybir.AxisListType
F32 = mybir.dt.float32
F16 = mybir.dt.float16
I32 = mybir.dt.int32

N, D = 1024, 512
TT, DC = N // P, D // P
LN_EPS = 1e-5


class Chain:

    def __init__(self, eng, sem):
        self.eng, self.sem, self.n = eng, sem, 0

    def __call__(self, ins):
        self.n += 1
        ins.then_inc(self.sem, 1)
        self.eng.wait_ge(self.sem, self.n)


class Kit:

    def __init__(self, nc):
        self.nc = nc

    def sb(self, ctx, name, shape, dt=F32):
        return ctx.enter_context(self.nc.sbuf_tensor(name, shape, dt))

    def ps(self, ctx, name, shape, dt=F32):
        return ctx.enter_context(self.nc.psum_tensor(name, shape, dt))

    def sem(self, ctx, name):
        return ctx.enter_context(self.nc.semaphore(name))


def rsqrt_steps(dve, step, out, var, eps, half, tmp):
    step(dve.tensor_scalar(half, var, eps, None, ALU.add))
    step(dve.tensor_scalar(tmp.bitcast(I32), half.bitcast(I32), 1, None, ALU.logical_shift_right))
    step(dve.tensor_scalar(out.bitcast(I32), tmp.bitcast(I32), -1.0, float(0x5F3759DF), ALU.mult, ALU.add))
    step(dve.tensor_scalar(half, half, -0.5, None, ALU.mult))
    for _ in range(4):
        step(dve.tensor_tensor(tmp, out, out, ALU.mult))
        step(dve.tensor_tensor(tmp, tmp, half, ALU.mult))
        step(dve.scalar_tensor_tensor(out, tmp, 1.5, out, ALU.add, ALU.mult))


def norm_rows(dve, step, x, xn, stats, mv, var, rstd, half, tmp):
    for t in range(TT):
        ins = dve.bn_stats(stats[:, t, :], x[:, t, :])
    step(ins)
    for t in range(TT):
        ins = dve.bn_aggr(mv[:, t, :], stats[:, t, :])
    step(ins)
    step(dve.tensor_copy(var, mv[:, :, 1]))
    rsqrt_steps(dve, step, rstd, var, LN_EPS, half, tmp)
    for t in range(TT):
        ins = dve.tensor_scalar(xn[:, t, :], x[:, t, :], mv[:, t, 0:1], rstd[:, t:t + 1], ALU.subtract, ALU.mult)
    return ins


E = 17408
EC = E // P
G = 4
ECP = EC + G


class Persistent:

    def __init__(self, kit, ctx, graph_ctx):
        sb = lambda *a: kit.sb(ctx, *a)
        self.x = sb("x", [P, TT, D])
        self.xn = sb("xn", [P, TT, D])
        self.xnT = sb("xnT", [P, DC, N])
        self.ident = sb("ident", [P, P])
        self.ones = sb("ones", [P, P])
        self.stats = sb("stats", [P, TT, 6])
        self.mv = sb("mv", [P, TT, 2])
        self.var = sb("var", [P, TT])
        self.rstd = sb("rstd", [P, TT])
        self.half = sb("half", [P, TT])
        self.tmp = sb("tmp", [P, TT])
        self.deg_in = kit.sb(graph_ctx, "deg_in", [P, TT])
        self.countT = kit.sb(graph_ctx, "countT", [P, TT, N])


def transpose_xn(pe, ps, st, xn_ready, evacuated, transposed, base=0, first_wait=1):
    pe.wait_ge(xn_ready, first_wait)
    for i in range(2 * DC):
        c, h = i // 2, i % 2
        if i >= 2:
            pe.wait_ge(evacuated, i - 1)
        for j in range(4):
            t = 4 * h + j
            ins = pe.transpose(ps[:, i % 2, j * P:(j + 1) * P], st.xn[:, t, c * P:(c + 1) * P], st.ident[:, :])
        ins.then_inc(transposed, 1)


def evacuate_xnT(act, ps, st, evacuated, transposed):
    for i in range(2 * DC):
        c, h = i // 2, i % 2
        act.wait_ge(transposed, i + 1)
        act.activation(st.xnT[:, c, h * 512:(h + 1) * 512], ps[:, i % 2, :], ACT.Copy).then_inc(evacuated, 1)


def stage_graph(kit, st, x, src, dst, weight, bias):
    nc = kit.nc
    with ExitStack() as ctx:
        sb = lambda *a: kit.sb(ctx, *a)
        sem = lambda n: kit.sem(ctx, n)
        count = sb("count", [P, TT, N])
        adj = sb("adj", [P, TT, N])
        wgt = sb("wgt", [P, DC, D])
        bias_bc = sb("bias_bc", [P, D])
        h = sb("h", [P, TT, D])
        rows_i = sb("rows_i", [P, 2, P], I32)
        tail_i = sb("tail_i", [EC - P, 2, P], I32)
        rows_f = sb("rows_f", [P, 2, P])
        tail_f = sb("tail_f", [EC - P, 2, P])
        ends = sb("ends", [P, 2, ECP])
        ends_local = sb("ends_local", [P, ECP])
        lowhigh = sb("lowhigh", [P, 2, 2])
        diag = sb("diag", [P, 2, 2, P])
        spans = sb("spans", [TT, 2, EC])
        iota_i = sb("iota_i", [P, N], I32)
        iota_f = sb("iota_f", [P, EC])
        iota_16 = sb("iota_16", [P, N], F16)
        zero_16 = sb("zero_16", [P, P], F16)
        limit_i = sb("limit_i", [P, 2], I32)
        limit = sb("limit", [P, 2])
        shift_i = sb("shift_i", [P, TT], I32)
        shift = sb("shift", [P, TT])
        touch = sb("touch", [TT, EC])
        pick = sb("pick", [TT, EC])
        lohi = sb("lohi", [TT, 4])
        table_f = sb("table_f", [1, 4, TT])
        table = sb("table", [1, 4, TT], I32)
        hot_src = sb("hot_src", [P, G, N], F16)
        hot_dst = sb("hot_dst", [P, G, P], F16)
        deg = sb("deg", [P, TT])
        dinv = sb("dinv", [P, TT])
        ps_c = kit.ps(ctx, "ps_c", [P, 2, N])
        ps_t = kit.ps(ctx, "ps_t", [P, 2, 512])
        ps_m = kit.ps(ctx, "ps_m", [P, 2, 512])

        edges_in, x_in, w_in = sem("edges_in"), sem("x_in"), sem("w_in")
        consts, localised = sem("consts"), sem("localised")
        dve_own = sem("dve_own")
        pool_own = sem("pool_own")
        rows_ready, rows_turned, ends_ready = sem("rows_ready"), sem("rows_turned"), sem("ends_ready")
        diag_ready, spans_there, lohi_ready = sem("diag_ready"), sem("spans_there"), sem("lohi_ready")
        table_moved, table_ready = sem("table_moved"), sem("table_ready")
        xn_ready, xnT_turned, xnT_ready = sem("xn_ready"), sem("xnT_turned"), sem("xnT_ready")
        h_done, h_ready = sem("h_done"), sem("h_ready")
        slots_free, slots_full = sem("slots_free"), sem("slots_full")
        bank_free, tile_counted, counts_ready = sem("bank_free"), sem("tile_counted"), sem("counts_ready")
        turned, turned_ready = sem("turned"), sem("turned_ready")
        adj_ready, scaled = sem("adj_ready"), sem("scaled")
        mixed, mixed_free = sem("mixed"), sem("mixed_free")

        with nc.Block() as block:
            @block.sync
            def _(sp):
                for i, ends_dram in enumerate((src, dst)):
                    chunks = ends_dram.rearrange("(c e) -> c e", e=P)
                    sp.dma_start(rows_i[:, i, :], chunks[0:P, :]).then_inc(edges_in, 16)
                    sp.dma_start(tail_i[:, i, :], chunks[P:EC, :]).then_inc(edges_in, 16)
                sp.dma_start(st.x[:, :, :], x.rearrange("(t p) d -> p t d", p=P)).then_inc(x_in, 16)
                sp.dma_start(wgt[:, :, :], weight.rearrange("(c p) n -> p c n", p=P)).then_inc(w_in, 16)
                sp.dma_start(bias_bc[:, :], bias.partition_broadcast(P)).then_inc(w_in, 16)
                sp.wait_ge(lohi_ready, 1)
                for i in range(2):
                    sp.dma_start(table_f[0:1, i, :], lohi[:, i:i + 1]).then_inc(table_moved, 16)

            @block.gpsimd
            def _(pool):
                step = Chain(pool, pool_own)
                step(pool.memset(st.ident[:, :], 0.0))
                step(pool.affine_select(out=st.ident[:, :], in_=st.ident[:, :], compare_op=ALU.not_equal, fill=1.0,
                                        base=0, pattern=[[-1, P]], channel_multiplier=1))
                pool.memset(st.ones[:, :], 1.0)
                pool.memset(zero_16[:, :], 0.0)
                pool.iota(iota_i[:, :], pattern=[[1, N]], base=0, channel_multiplier=0)
                pool.iota(limit_i[:, 0:1], pattern=[[0, 1]], base=0, channel_multiplier=P)
                pool.iota(limit_i[:, 1:2], pattern=[[0, 1]], base=P - 1, channel_multiplier=P)
                pool.memset(ends[:, :, EC:ECP], -1.0)
                pool.iota(shift_i[:, :], pattern=[[P, TT]], base=0, channel_multiplier=0).then_inc(consts, 1)

            @block.vector
            def _(dve):
                step = Chain(dve, dve_own)
                dve.wait_ge(consts, 1)
                dve.tensor_copy(iota_16[:, :], iota_i[:, :])
                dve.tensor_copy(iota_f[:, :], iota_i[:, 0:EC])
                dve.tensor_copy(limit[:, :], limit_i[:, :])
                step(dve.tensor_copy(shift[:, :], shift_i[:, :]))
                dve.wait_ge(edges_in, 64)
                dve.tensor_copy(rows_f[:, :, :], rows_i[:, :, :])
                dve.tensor_copy(tail_f[:, :, :], tail_i[:, :, :]).then_inc(rows_ready, 1)
                dve.wait_ge(rows_ready, 1)
                for b, rows, n in ((0, rows_f, P), (1, tail_f, EC - P)):
                    for i, op in enumerate((ALU.min, ALU.max)):
                        ins = dve.tensor_reduce(lowhigh[0:n, b, i:i + 1], rows[:, 1, :], AX.X, op)
                step(ins)
                for b, n in ((0, P), (1, EC - P)):
                    for i in range(2):
                        ins = dve.tensor_scalar(diag[0:n, b, i, 0:n], st.ident[0:n, 0:n], lowhigh[0:n, b, i:i + 1],
                                                None, ALU.mult)
                ins.then_inc(diag_ready, 1)
                dve.wait_ge(rows_turned, 1)
                for i in range(2):
                    ins = dve.tensor_copy(ends[:, i, 0:EC], ps_t[:, i, 0:EC])
                step(ins)
                dve.wait_ge(spans_there, 1)
                step(dve.tensor_copy(spans[:, :, :], ps_m[0:TT, 0, 0:2 * EC].rearrange("m (i c) -> m i c", i=2)))
                step(dve.tensor_scalar(touch[:, :], spans[:, 0, :], limit[0:TT, 1:2], None, ALU.is_le))
                step(dve.scalar_tensor_tensor(touch[:, :], spans[:, 1, :], limit[0:TT, 0:1], touch[:, :],
                                              ALU.is_ge, ALU.mult))
                step(dve.tensor_tensor(pick[:, :], touch[:, :], iota_f[0:TT, :], ALU.mult))
                step(dve.tensor_reduce(lohi[:, 1:2], pick[:, :], AX.X, ALU.max))
                step(dve.scalar_tensor_tensor(pick[:, :], touch[:, :], -1000.0, iota_f[0:TT, :], ALU.mult, ALU.add))
                step(dve.tensor_reduce(lohi[:, 0:1], pick[:, :], AX.X, ALU.min))
                step(dve.tensor_scalar(lohi[:, 0:1], lohi[:, 0:1], 1000.0, lohi[:, 1:2], ALU.add, ALU.min))
                step(dve.tensor_scalar(lohi[:, 2:3], lohi[:, 1:2], lohi[:, 0:1], 1.0, ALU.subtract, ALU.add))
                step(dve.tensor_scalar(pick[:, 0:EC // G], iota_f[0:TT, 0:EC:G], lohi[:, 2:3], None, ALU.is_lt))
                dve.tensor_reduce(lohi[:, 1:2], pick[:, 0:EC // G], AX.X, ALU.add).then_inc(lohi_ready, 1)

                dve.wait_ge(x_in, 16)
                norm_rows(dve, step, st.x, st.xn, st.stats, st.mv, st.var[:, :], st.rstd[:, :], st.half[:, :],
                          st.tmp[:, :]).then_inc(xn_ready, 1)

                dve.wait_ge(table_moved, 32)
                step(dve.tensor_tensor_scan(table_f[0:1, 3, :], st.ones[0:1, 0:TT], table_f[0:1, 1, :], 0.0,
                                            ALU.mult, ALU.add))
                step(dve.tensor_tensor(table_f[0:1, 2, :], table_f[0:1, 3, :], table_f[0:1, 1, :], ALU.subtract))
                dve.tensor_copy(table[0:1, :, :], table_f[0:1, :, :]).then_inc(table_ready, 1)
                dve.wait_ge(table_ready, 1)
                with dve.Fori(0, TT) as m:
                    first = dve.value_load(table[0:1, 0, bass.ds(m, 1)], min_val=0, max_val=EC - 1)
                    groups = dve.value_load(table[0:1, 1, bass.ds(m, 1)], min_val=1, max_val=EC // G)
                    before = dve.value_load(table[0:1, 2, bass.ds(m, 1)], min_val=0, max_val=TT * EC // G)
                    dve.wait_ge(slots_free, (before + 1) * G)
                    dve.tensor_scalar(ends_local[:, :], ends[:, 1, :], shift[:, bass.ds(m, 1)], None,
                                      ALU.subtract).then_inc(localised, 1)
                    with dve.Fori(0, groups) as j:
                        chunk = (first + j * G).with_bounds(min_val=0, max_val=EC - 1)
                        for i in range(G):
                            dve.wait_ge(slots_free, (before + j) * G + (i + 1))
                            c = chunk + i
                            if i == 0:
                                dve.wait_ge(localised, m + 1)
                            dve.tensor_scalar(hot_dst[:, i, :], iota_16[:, 0:P], ends_local[:, bass.ds(c, 1)],
                                              None, ALU.is_equal)
                            dve.tensor_scalar(hot_src[:, i, :], iota_16[:, :], ends[:, 0, bass.ds(c, 1)],
                                              None, ALU.is_equal).then_inc(slots_full, 1)

                dve.wait_ge(counts_ready, TT)
                step(dve.tensor_reduce(st.deg_in[:, :], count[:, :, :], AX.X, ALU.add))
                for t in range(TT):
                    dve.wait_ge(turned_ready, 2 * t + 2)
                    step(dve.scalar_tensor_tensor(adj[:, t, :], count[:, t, :], 0.0, st.countT[:, t, :],
                                                  ALU.is_gt, ALU.max))
                    step(dve.tensor_scalar(adj[:, t, :], adj[:, t, :], 1.0, None, ALU.min))
                    step(dve.tensor_tensor(adj[:, t, t * P:(t + 1) * P], adj[:, t, t * P:(t + 1) * P],
                                           st.ident[:, :], ALU.add))
                step(dve.tensor_reduce(deg[:, :], adj[:, :, :], AX.X, ALU.add))
                rsqrt_steps(dve, step, dinv[:, :], deg[:, :], 0.0, st.half[:, :], st.tmp[:, :])
                dve.wait_ge(h_ready, TT)
                for t in range(TT):
                    ins = dve.tensor_scalar(h[:, t, :], h[:, t, :], dinv[:, t:t + 1], None, ALU.mult)
                ins.then_inc(adj_ready, 1)
                for t in range(TT):
                    ins = dve.tensor_tensor(st.x[:, t, :], st.x[:, t, :], bias_bc[:, :], ALU.add)
                step(ins)
                for t in range(TT):
                    dve.wait_ge(mixed, t + 1)
                    dve.scalar_tensor_tensor(st.x[:, t, :], ps_m[:, t % 2, :], dinv[:, t:t + 1], st.x[:, t, :],
                                             ALU.mult, ALU.add).then_inc(mixed_free, 1)

            @block.tensor
            def _(pe):
                pe.wait_ge(rows_ready, 1)
                for i in range(2):
                    pe.transpose(ps_t[:, i, 0:P], rows_f[:, i, :], st.ident[:, :])
                    ins = pe.transpose(ps_t[:, i, P:EC], tail_f[:, i, :], st.ident[0:EC - P, 0:EC - P])
                ins.then_inc(rows_turned, 1)
                pe.wait_ge(diag_ready, 1)
                for i in range(2):
                    pe.matmul(ps_m[0:TT, 0, i * EC:i * EC + P], st.ones[:, 0:TT], diag[:, 0, i, :],
                              start=True, stop=True)
                    ins = pe.matmul(ps_m[0:TT, 0, i * EC + P:(i + 1) * EC], st.ones[0:EC - P, 0:TT],
                                    diag[0:EC - P, 1, i, 0:EC - P], start=True, stop=True)
                ins.then_inc(spans_there, 1)
                pe.wait_ge(dve_own, 2)
                transpose_xn(pe, ps_t, st, xn_ready, xnT_ready, xnT_turned)
                pe.wait_ge(xnT_ready, 2 * DC)
                pe.wait_ge(w_in, 32)
                pe.wait_ge(lohi_ready, 1)
                for t in range(TT):
                    if t >= 2:
                        pe.wait_ge(h_ready, t - 1)
                    for c in range(DC):
                        ins = pe.matmul(ps_m[:, t % 2, :], st.xnT[:, c, t * P:(t + 1) * P], wgt[:, c, :],
                                        start=c == 0, stop=c == DC - 1)
                    ins.then_inc(h_done, 1)
                pe.nop().then_inc(slots_free, G)
                pe.wait_ge(table_ready, 1)
                with pe.Fori(0, TT // 2) as pair:
                    for b in range(2):
                        m = pair * 2 + b
                        groups = pe.value_load(table[0:1, 1, bass.ds(m, 1)], min_val=1, max_val=EC // G)
                        before = pe.value_load(table[0:1, 2, bass.ds(m, 1)], min_val=0, max_val=TT * EC // G)
                        pe.wait_ge(bank_free, m + 1)
                        for q in range(2):
                            pe.matmul(ps_c[:, b, q * 512:(q + 1) * 512], zero_16[:, :], iota_16[:, 0:512],
                                      start=True, stop=False, skip_group_check=True)
                        with pe.Fori(0, groups) as j:
                            for i in range(G):
                                pe.wait_ge(slots_full, (before + j) * G + (i + 1))
                                for q in range(2):
                                    ins = pe.matmul(ps_c[:, b, q * 512:(q + 1) * 512], hot_dst[:, i, :],
                                                    hot_src[:, i, q * 512:(q + 1) * 512],
                                                    start=False, stop=False, skip_group_check=True)
                                ins.then_inc(slots_free, 1)
                        for q in range(2):
                            ins = pe.matmul(ps_c[:, b, q * 512:(q + 1) * 512], zero_16[:, :], iota_16[:, 0:512],
                                            start=False, stop=True, skip_group_check=True)
                        ins.then_inc(tile_counted, 1)
                for i in range(2 * TT):
                    s, half = i // 2, i % 2
                    pe.wait_ge(counts_ready, TT)
                    if i >= 2:
                        pe.wait_ge(turned_ready, i - 1)
                    for j in range(4):
                        ins = pe.transpose(ps_t[:, i % 2, j * P:(j + 1) * P],
                                           count[:, 4 * half + j, s * P:(s + 1) * P], st.ident[:, :])
                    ins.then_inc(turned, 1)
                pe.wait_ge(adj_ready, 1)
                for t in range(TT):
                    if t >= 2:
                        pe.wait_ge(mixed_free, t - 1)
                    for s in range(TT):
                        ins = pe.matmul(ps_m[:, t % 2, :], adj[:, s, t * P:(t + 1) * P], h[:, s, :],
                                        start=s == 0, stop=s == TT - 1)
                    ins.then_inc(mixed, 1)

            @block.scalar
            def _(act):
                evacuate_xnT(act, ps_t, st, xnT_ready, xnT_turned)
                for t in range(TT):
                    act.wait_ge(h_done, t + 1)
                    act.activation(h[:, t, :], ps_m[:, t % 2, :], ACT.Copy).then_inc(h_ready, 1)
                act.nop().then_inc(bank_free, 2)
                with act.Fori(0, TT // 2) as pair:
                    for b in range(2):
                        m = pair * 2 + b
                        act.wait_ge(tile_counted, m + 1)
                        act.activation(count[:, bass.ds(m, 1), :], ps_c[:, b:b + 1, :],
                                       ACT.Copy).then_inc(bank_free, 1)
                        act.wait_ge(bank_free, m + 3)
                        act.nop().then_inc(counts_ready, 1)
                for i in range(2 * TT):
                    s, half = i // 2, i % 2
                    act.wait_ge(turned, i + 1)
                    act.activation(st.countT[:, s, half * 512:(half + 1) * 512], ps_t[:, i % 2, :],
                                   ACT.Copy).then_inc(turned_ready, 1)


EX, F, TOPK = 16, 1024, 2
FC = F // P
MAXT = N * TOPK // P + EX - 1
LISTS = 32
STEPS = 20


class LoopChain:

    def __init__(self, eng, sem, start):
        self.eng, self.sem, self.start, self.n = eng, sem, start, 0

    def __call__(self, ins):
        self.n += 1
        ins.then_inc(self.sem, 1)
        self.eng.wait_ge(self.sem, self.start + self.n)


def stage_moe(kit, st, gate_w, gate_b, w1, b1, w2, b2, gamma, beta):
    nc = kit.nc
    xn_dram = nc.dram_tensor("xn_dram", (N, D), F32, kind="Internal").ap()
    y_dram = nc.dram_tensor("y_dram", ((MAXT + 2) * P, D), F32, kind="Internal").ap()
    with ExitStack() as outer:
        weight = kit.sb(outer, "weight", [P, TT, TOPK])
        place = kit.sb(outer, "place", [P, TOPK, TT], mybir.dt.uint32)
        rowlist = kit.sb(outer, "rowlist", [P, LISTS], mybir.dt.uint32)
        table = kit.sb(outer, "table_moe", [1, 2, EX], I32)
        b1T = kit.sb(outer, "b1T", [P, EX * FC])
        with ExitStack() as ctx:
            sb = lambda *a: kit.sb(ctx, *a)
            sem = lambda n: kit.sem(ctx, n)
            gw = sb("gw", [P, DC, EX])
            gb = sb("gb", [P, EX])
            b1_rows = sb("b1_rows", [P, P])
            iota_i = sb("iota_i2", [P, P], I32)
            iota = sb("iota2", [P, P])
            node_i = sb("node_i", [P, TT], I32)
            node = sb("node", [P, TT])
            before = sb("before", [P, P])
            score = sb("score", [P, TT, EX])
            best = sb("best", [P, TT, 8])
            which = sb("which", [P, TT, 8], mybir.dt.uint32)
            which_f = sb("which_f", [P, TT, TOPK])
            hot = sb("hot", [P, TOPK, TT, EX])
            both = sb("both", [P, TT, EX])
            totals = sb("totals", [P, TT + 1, EX])
            rank = sb("rank", [P, TT, EX])
            tiles = sb("tiles", [P, EX])
            upto = sb("upto", [P, EX])
            start = sb("start", [P, EX])
            gap = sb("gap", [P, TT])
            ratio = sb("ratio", [P, TT])
            slot = sb("slot", [P, TOPK, TT])
            slot_i = sb("slot_i", [P, TOPK, TT], I32)
            part_i = sb("part_i", [P, 2, TOPK, TT], I32)
            part = sb("part", [P, 2, TOPK, TT])
            hot_row = sb("hot_row", [P, TOPK, TT, P])
            hot_tile = sb("hot_tile", [P, TOPK, TT, LISTS])
            ps_t = kit.ps(ctx, "ps_t2", [P, 2, 512])
            ps_s = kit.ps(ctx, "ps_s", [P, TT, EX])
            ps_r = kit.ps(ctx, "ps_r", [P, 512])
            ps_n = kit.ps(ctx, "ps_n", [P, 512])
            ps_l = kit.ps(ctx, "ps_l", [P, 512])

            consts, loaded = sem("consts3"), sem("loaded3")
            dve_own, pool_own = sem("dve_own3"), sem("pool_own3")
            xn_ready, xnT_turned, xnT_ready = sem("xn_ready3"), sem("xnT_turned3"), sem("xnT_ready3")
            xn_stored = sem("xn_stored")
            b1_turned, scored = sem("b1_turned"), sem("scored")
            gap_ready, ratio_ready = sem("gap_ready"), sem("ratio_ready")
            both_ready, ranked = sem("both_ready"), sem("ranked")
            hots_ready, listed = sem("hots_ready"), sem("listed")

            with nc.Block() as block:
                @block.sync
                def _(sp):
                    sp.dma_start(gw[:, :, :], gate_w.rearrange("(c p) e -> p c e", p=P)).then_inc(loaded, 16)
                    sp.dma_start(gb[:, :], gate_b.partition_broadcast(P)).then_inc(loaded, 16)
                    sp.dma_start(b1_rows[:, :], b1.rearrange("e (f p) -> (e f) p", p=P)).then_inc(loaded, 16)
                    sp.wait_ge(xn_ready, 1)
                    sp.dma_start(xn_dram.rearrange("(t p) d -> p t d", p=P), st.xn[:, :, :]).then_inc(xn_stored, 16)
                    sp.wait_ge(xn_stored, 16)

                @block.gpsimd
                def _(pool):
                    step = Chain(pool, pool_own)
                    pool.iota(iota_i[:, :], pattern=[[1, P]], base=0, channel_multiplier=0)
                    pool.iota(node_i[:, :], pattern=[[P, TT]], base=0, channel_multiplier=1)
                    step(pool.memset(before[:, :], 1.0))
                    pool.affine_select(out=before[:, :], in_=before[:, :], compare_op=ALU.is_ge, fill=0.0,
                                       base=-1, pattern=[[1, P]], channel_multiplier=-1).then_inc(consts, 1)

                @block.vector
                def _(dve):
                    step = Chain(dve, dve_own)
                    norm_rows(dve, step, st.x, st.xn, st.stats, st.mv, st.var[:, :], st.rstd[:, :], st.half[:, :],
                              st.tmp[:, :]).then_inc(xn_ready, 1)
                    dve.wait_ge(consts, 1)
                    dve.tensor_copy(iota[:, :], iota_i[:, :])
                    step(dve.tensor_copy(node[:, :], node_i[:, :]))
                    dve.wait_ge(b1_turned, 1)
                    dve.tensor_copy(b1T[:, :], ps_l[:, 0:EX * FC])
                    dve.wait_ge(scored, 1)
                    step(dve.tensor_tensor(score[:, :, :], ps_s[:, :, :],
                                           gb[:, :].unsqueeze(1).broadcast_to([P, TT, EX]), ALU.add))
                    for t in range(TT):
                        ins = dve.max(best[:, t, :], score[:, t, :])
                    step(ins)
                    for t in range(TT):
                        dve.max_index(which[:, t, :], best[:, t, :], score[:, t, :])
                    dve.tensor_tensor(gap[:, :], best[:, :, 1], best[:, :, 0], ALU.subtract).then_inc(gap_ready, 1)
                    dve.wait_ge(gap_ready, 1)
                    step(dve.tensor_copy(which_f[:, :, :], which[:, :, 0:TOPK]))
                    for k in range(TOPK):
                        ins = dve.tensor_tensor(hot[:, k, :, :],
                                                iota[:, 0:EX].unsqueeze(1).broadcast_to([P, TT, EX]),
                                                which_f[:, :, k].unsqueeze(2).broadcast_to([P, TT, EX]),
                                                ALU.is_equal)
                    step(ins)
                    dve.tensor_tensor(both[:, :, :], hot[:, 0, :, :], hot[:, 1, :, :], ALU.add).then_inc(both_ready, 1)
                    dve.wait_ge(ratio_ready, 1)
                    step(dve.tensor_scalar(gap[:, :], ratio[:, :], 1.0, None, ALU.add))
                    step(dve.reciprocal(gap[:, :], gap[:, :]))
                    dve.tensor_copy(weight[:, :, 0], gap[:, :])
                    dve.tensor_tensor(weight[:, :, 1], gap[:, :], ratio[:, :], ALU.mult)
                    dve.wait_ge(ranked, 1)
                    step(dve.memset(totals[:, 0, :], 0.0))
                    for t in range(TT):
                        step(dve.tensor_tensor(totals[:, t + 1, :], totals[:, t, :], ps_n[:, t * EX:(t + 1) * EX],
                                               ALU.add))
                    dve.tensor_tensor(rank[:, :, :], totals[:, 0:TT, :],
                                      ps_r[:, 0:TT * EX].rearrange("p (t e) -> p t e", e=EX), ALU.add)
                    step(dve.memset(tiles[:, :], 1.0))
                    for k in range(1, TT):
                        step(dve.scalar_tensor_tensor(tiles[:, :], totals[:, TT, :], float(k * P), tiles[:, :],
                                                      ALU.is_gt, ALU.add))
                    step(dve.tensor_tensor_scan(upto[:, :], st.ones[:, 0:EX], tiles[:, :], 0.0, ALU.mult, ALU.add))
                    step(dve.tensor_tensor(start[:, :], upto[:, :], tiles[:, :], ALU.subtract))
                    dve.tensor_copy(table[0:1, 0, :], tiles[0:1, :])
                    dve.tensor_copy(table[0:1, 1, :], start[0:1, :])
                    step(dve.scalar_tensor_tensor(rank[:, :, :], start[:, :].unsqueeze(1).broadcast_to([P, TT, EX]),
                                                  float(P), rank[:, :, :], ALU.mult, ALU.add))
                    for k in range(TOPK):
                        ins = dve.tensor_tensor(hot[:, k, :, :], hot[:, k, :, :], rank[:, :, :], ALU.mult)
                    step(ins)
                    step(dve.tensor_reduce(slot[:, :, :], hot[:, :, :, :], AX.X, ALU.add))
                    step(dve.tensor_copy(slot_i[:, :, :], slot[:, :, :]))
                    dve.tensor_scalar(part_i[:, 0, :, :], slot_i[:, :, :], P - 1, None, ALU.bitwise_and)
                    dve.tensor_scalar(part_i[:, 1, :, :], slot_i[:, :, :], 7, None, ALU.logical_shift_right)
                    step(dve.tensor_scalar(place[:, :, :], slot[:, :, :], float(P), None, ALU.add))
                    step(dve.tensor_copy(part[:, :, :, :], part_i[:, :, :, :]))
                    for k in range(TOPK):
                        for t in range(TT):
                            dve.tensor_scalar(hot_row[:, k, t, :], iota[:, :], part[:, 0, k, t:t + 1], None,
                                              ALU.is_equal)
                            ins = dve.tensor_scalar(hot_tile[:, k, t, :], iota[:, 0:LISTS], part[:, 1, k, t:t + 1],
                                                    node[:, t:t + 1], ALU.is_equal, ALU.mult)
                    ins.then_inc(hots_ready, 1)
                    dve.wait_ge(listed, 1)
                    dve.tensor_copy(rowlist[:, :], ps_l[:, 256:256 + LISTS])

                @block.tensor
                def _(pe):
                    pe.wait_ge(loaded, 48)
                    pe.transpose(ps_l[:, 0:P], b1_rows[:, :], st.ident[:, :]).then_inc(b1_turned, 1)
                    transpose_xn(pe, ps_t, st, xn_ready, xnT_ready, xnT_turned)
                    pe.wait_ge(xnT_ready, 2 * DC)
                    for t in range(TT):
                        for c in range(DC):
                            ins = pe.matmul(ps_s[:, t, :], st.xnT[:, c, t * P:(t + 1) * P], gw[:, c, :],
                                            start=c == 0, stop=c == DC - 1)
                    ins.then_inc(scored, 1)
                    pe.wait_ge(both_ready, 1)
                    pe.wait_ge(consts, 1)
                    flat = both[:, :, :].rearrange("p t e -> p (t e)")
                    pe.matmul(ps_r[:, 0:TT * EX], before[:, :], flat, start=True, stop=True)
                    pe.matmul(ps_n[:, 0:TT * EX], st.ones[:, :], flat, start=True, stop=True).then_inc(ranked, 1)
                    pe.wait_ge(hots_ready, 1)
                    for k in range(TOPK):
                        for t in range(TT):
                            ins = pe.matmul(ps_l[:, 256:256 + LISTS], hot_row[:, k, t, :], hot_tile[:, k, t, :],
                                            start=k == 0 and t == 0, stop=k == TOPK - 1 and t == TT - 1)
                    ins.then_inc(listed, 1)

                @block.scalar
                def _(act):
                    evacuate_xnT(act, ps_t, st, xnT_ready, xnT_turned)
                    act.wait_ge(gap_ready, 1)
                    act.activation(ratio[:, :], gap[:, :], ACT.Exp).then_inc(ratio_ready, 1)

        with ExitStack() as ctx:
            sb = lambda *a: kit.sb(ctx, *a)
            sem = lambda n: kit.sem(ctx, n)
            w1_sb = sb("w1_sb", [P, 2, DC, F])
            w2_sb = sb("w2_sb", [P, 2, FC, D])
            affine = sb("affine", [P, 2, 3, D])
            index = sb("index", [P, 1], mybir.dt.uint32)
            rows = sb("rows", [P, D])
            rowsT = sb("rowsT", [P, DC, P])
            hT = sb("hT", [P, FC, P])
            y = sb("y", [P, D])
            y_out = sb("y_out", [P, D])
            zeros = sb("zeros", [P, D])
            stat = sb("stat", [P, 6])
            mean = sb("mean", [P, 2])
            rs = sb("rs", [P, 3])
            ps_x = kit.ps(ctx, "ps_x", [P, DC, P])
            ps_h = kit.ps(ctx, "ps_h", [P, FC, P])
            ps_y = kit.ps(ctx, "ps_y", [P, D])

            w1_in = [sem("w1_in0"), sem("w1_in1")]
            w2_in = [sem("w2_in0"), sem("w2_in1")]
            affine_in = [sem("affine_in0"), sem("affine_in1")]
            index_ready = sem("index_ready")
            rows_in, rows_turned, rowsT_ready = sem("rows_in"), sem("rows_turned3"), sem("rowsT_ready")
            h_done, hT_ready = sem("h_done3"), sem("hT_ready")
            y_done, y_taken = sem("y_done"), sem("y_taken")
            y_ready, y_stored = sem("y_ready"), sem("y_stored")
            own = sem("own3")
            zeros_ready, zeros_stored = sem("zeros_ready"), sem("zeros_stored")

            def expert(eng, pair, b):
                e = pair * 2 + b
                tiles = eng.value_load(table[0:1, 0, bass.ds(e, 1)], min_val=1, max_val=TT)
                before = eng.value_load(table[0:1, 1, bass.ds(e, 1)], min_val=0, max_val=MAXT - 1)
                return e, tiles, before

            with nc.Block() as block:
                @block.sync
                def _(sp):
                    def load(e, b):
                        sp.dma_start(w1_sb[:, b, :, :], w1[bass.ds(e, 1)].rearrange("e (c p) f -> p (e c) f", p=P)
                                     ).then_inc(w1_in[b], 16)
                        for i, v in enumerate((b2, gamma, beta)):
                            sp.dma_start(affine[:, b, i, :], v[bass.ds(e, 1)].rearrange("e d -> (e d)")
                                         .partition_broadcast(P)).then_inc(affine_in[b], 16)
                        sp.dma_start(w2_sb[:, b, :, :], w2[bass.ds(e, 1)].rearrange("e (f p) d -> p (e f) d", p=P)
                                     ).then_inc(w2_in[b], 16)
                    for b in range(2):
                        load(b, b)
                    _, n, before = expert(sp, EX // 2 - 1, 1)
                    sp.wait_ge(zeros_ready, 1)
                    with sp.Fori(0, before * -1 - n + (MAXT + 1)) as i:
                        tile = (before + n + 1 + i).with_bounds(min_val=0, max_val=MAXT + 1)
                        sp.dma_start(y_dram[bass.ds(tile * P, P), :], zeros[:, :]).then_inc(zeros_stored, 16)
                        sp.wait_ge(zeros_stored, (i + 1) * 16)
                    with sp.Fori(0, EX // 2 - 1) as pair:
                        for b in range(2):
                            e, tiles, before = expert(sp, pair, b)
                            sp.wait_ge(y_ready, before + tiles + 1)
                            load(e + 2, b)

                @block.gpsimd
                def _(pool):
                    last = pool.value_load(table[0:1, 1, EX - 1:EX], min_val=0, max_val=MAXT - 1)
                    n = pool.value_load(table[0:1, 0, EX - 1:EX], min_val=1, max_val=TT)
                    with pool.Fori(0, last + n + 1) as g:
                        pool.wait_ge(rows_turned, g + 1)
                        pool.tensor_copy(index[:, :], rowlist[:, bass.ds(g.with_bounds(min_val=0, max_val=LISTS - 1), 1)]).then_inc(index_ready, 1)
                        pool.wait_ge(index_ready, 1)
                        pool.wait_ge(index_ready, g + 1)
                        pool.indirect_dma_start(out=rows[:, :], out_offset=None, in_=xn_dram,
                                                in_offset=bass.IndirectOffsetOnAxis(ap=index[:, :], axis=0)
                                                ).then_inc(rows_in, 16)

                @block.tensor
                def _(pe):
                    def turn(g):
                        pe.wait_ge(rows_in, (g + 1) * 16)
                        for c in range(DC):
                            ins = pe.transpose(ps_x[:, c, :], rows[:, c * P:(c + 1) * P], st.ident[:, :])
                        ins.then_inc(rows_turned, 1)
                    pe.nop().then_inc(rows_turned, 1)
                    turn(0)
                    with pe.Fori(0, EX // 2) as pair:
                        for b in range(2):
                            _, tiles, before = expert(pe, pair, b)
                            with pe.Fori(0, tiles) as j:
                                g = before + j
                                pe.wait_ge(w1_in[b], (pair + 1) * 16)
                                pe.wait_ge(rowsT_ready, g + 1)
                                for f in range(FC):
                                    if f % 4 == 0:
                                        pe.wait_ge(hT_ready, (g + 1) * 2 + (f // 4 - 1))
                                    for c in range(DC):
                                        ins = pe.matmul(ps_h[:, f, :], w1_sb[:, b, c, f * P:(f + 1) * P],
                                                        rowsT[:, c, :], start=c == 0, stop=c == DC - 1)
                                    if f % 4 == 3:
                                        ins.then_inc(h_done, 1)
                                turn(g + 1)
                                pe.wait_ge(w2_in[b], (pair + 1) * 16)
                                pe.wait_ge(y_taken, g + 1)
                                for f in range(FC):
                                    if f % 4 == 0:
                                        pe.wait_ge(hT_ready, (g + 1) * 2 + (f // 4 + 1))
                                    ins = pe.matmul(ps_y[:, :], hT[:, f, :], w2_sb[:, b, f, :],
                                                    start=f == 0, stop=f == FC - 1)
                                ins.then_inc(y_done, 1)

                @block.scalar
                def _(act):
                    def take_rows(g):
                        act.wait_ge(rows_turned, g + 2)
                        act.activation(rowsT[:, :, :], ps_x[:, :, :], ACT.Copy).then_inc(rowsT_ready, 1)

                    def store(g):
                        act.wait_ge(y_ready, g + 1)
                        act.dma_start(y_dram[bass.ds(g * P, P), :], y_out[:, :]).then_inc(y_stored, 16)
                    act.nop().then_inc(hT_ready, 2)
                    take_rows(0)
                    with act.Fori(0, EX // 2) as pair:
                        for b in range(2):
                            e, tiles, before = expert(act, pair, b)
                            with act.Fori(0, tiles) as j:
                                g = (before + j).with_bounds(min_val=0, max_val=MAXT - 1)
                                for f in range(FC):
                                    if f % 4 == 0:
                                        act.wait_ge(h_done, g * 2 + (f // 4 + 1))
                                        act.wait_ge(y_done, g + 1)
                                    ins = act.activation(hT[:, f, :], ps_h[:, f, :], ACT.Gelu,
                                                         bias=b1T[:, bass.ds(e * FC + f, 1)])
                                    if f % 4 == 3:
                                        ins.then_inc(hT_ready, 1)
                                take_rows(g + 1)
                                store(g)
                    _, n, last = expert(act, EX // 2 - 1, 1)
                    store((last + n).with_bounds(min_val=1, max_val=MAXT))
                    act.wait_ge(y_stored, (last + n + 1) * 16)
                    act.activation(hT[:, 0, 0:1], hT[:, 0, 0:1], ACT.Copy)

                @block.vector
                def _(dve):
                    dve.memset(zeros[:, :], 0.0).then_inc(zeros_ready, 1)
                    dve.memset(y_out[:, :], 0.0).then_inc(y_ready, 1)
                    dve.nop().then_inc(y_taken, 1)
                    dve.nop().then_inc(y_done, 1)
                    with dve.Fori(0, EX // 2) as pair:
                        for b in range(2):
                            _, tiles, before = expert(dve, pair, b)
                            with dve.Fori(0, tiles) as j:
                                g = before + j
                                step = LoopChain(dve, own, g * STEPS)
                                dve.wait_ge(affine_in[b], (pair + 1) * 48)
                                dve.wait_ge(y_done, g + 2)
                                ins = dve.tensor_tensor(y[:, :], ps_y[:, :], affine[:, b, 0, :], ALU.add)
                                ins.then_inc(y_taken, 1)
                                dve.wait_ge(y_taken, g + 2)
                                step(dve.bn_stats(stat[:, :], y[:, :]))
                                dve.memset(rs[:, 0:1], 0.0)
                                step(dve.bn_aggr(mean[:, :], stat[:, :]))
                                rsqrt_steps(dve, step, rs[:, 0:1], mean[:, 1:2], LN_EPS, rs[:, 1:2], rs[:, 2:3])
                                step(dve.tensor_scalar(y[:, :], y[:, :], mean[:, 0:1], rs[:, 0:1],
                                                       ALU.subtract, ALU.mult))
                                step(dve.tensor_tensor(y[:, :], y[:, :], affine[:, b, 1, :], ALU.mult))
                                dve.wait_ge(y_stored, (g + 1) * 16)
                                ins = dve.tensor_tensor(y_out[:, :], y[:, :], affine[:, b, 2, :], ALU.add)
                                ins.then_inc(y_ready, 1)
                                dve.wait_ge(y_ready, g + 2)
                                assert step.n == STEPS

        with ExitStack() as ctx:
            sem = lambda n: kit.sem(ctx, n)
            taken = kit.sb(ctx, "taken", [P, TOPK, TT, D])
            rows_in = [sem(f"rows_in4_{t}") for t in range(TT)]
            own = sem("own4")
            with nc.Block() as block:
                @block.gpsimd
                def _(pool):
                    for t in range(TT):
                        for k in range(TOPK):
                            pool.indirect_dma_start(out=taken[:, k, t, :], out_offset=None, in_=y_dram,
                                                    in_offset=bass.IndirectOffsetOnAxis(
                                                        ap=place[:, k, t:t + 1], axis=0)).then_inc(rows_in[t], 16)

                @block.vector
                def _(dve):
                    step = Chain(dve, own)
                    for t in range(TT):
                        dve.wait_ge(rows_in[t], 32)
                        for k in range(TOPK):
                            step(dve.scalar_tensor_tensor(st.x[:, t, :], taken[:, k, t, :], weight[:, t, k:k + 1],
                                                          st.x[:, t, :], ALU.mult, ALU.add))


GX, LAYERS = 4, 2


def stage_sage(kit, st, gate_w, gate_b, wl, bl, wr):
    nc = kit.nc
    with ExitStack() as ctx:
        sb = lambda *a: kit.sb(ctx, *a)
        sem = lambda n: kit.sem(ctx, n)
        gw = sb("gw5", [P, DC, GX])
        gb = sb("gb5", [P, GX])
        iota_i = sb("iota_i5", [P, GX], I32)
        iota = sb("iota5", [P, GX])
        prob = sb("prob", [P, TT, 8])
        best = sb("best5", [P, TT, 8])
        which = sb("which5", [P, TT, 8], mybir.dt.uint32)
        which_f = sb("which_f5", [P, TT, TOPK])
        pick = sb("pick5", [P, TT, GX])
        gate = sb("gate", [P, TT, GX])
        peak = sb("peak", [P, TT])
        inv = sb("inv", [P, TT])
        diag = sb("diag5", [P, TT, P])
        inv_bc = sb("inv_bc", [P, N])
        meanT = sb("meanT", [P, DC, N])
        h = sb("h5", [P, TT, D])
        hT = sb("hT5", [P, DC, N])
        mean2T = sb("mean2T", [P, DC, N])
        w = sb("w5", [P, LAYERS, 2, DC, D])
        bias = sb("bias5", [P, LAYERS, D])
        ps_t = kit.ps(ctx, "ps_t5", [P, 2, 512])
        ps_a = kit.ps(ctx, "ps_a", [P, 2, 512])
        ps_z = kit.ps(ctx, "ps_z", [P, 2, 512])
        ps_g = kit.ps(ctx, "ps_g", [P, TT, GX])

        w_in = [sem("w_in5_0"), sem("w_in5_1")]
        loaded, consts = sem("loaded5"), sem("consts5")
        own, loop_own = sem("own5"), sem("loop_own5")
        xn_ready, xnT_turned, xnT_ready = sem("xn_ready5"), sem("xnT_turned5"), sem("xnT_ready5")
        scored, logits, exp_done = sem("scored5"), sem("logits5"), sem("exp_done5")
        diag_ready, inv_spread = sem("diag_ready5"), sem("inv_spread")
        sum_done, sum_taken = sem("sum_done"), sem("sum_taken")
        z_done, z_taken = sem("z_done"), sem("z_taken")
        h_ready, h_turned, hT_taken = sem("h_ready5"), sem("h_turned5"), sem("hT_taken5")
        OWN = TT

        def load_layer(eng, e, l):
            for i, m in enumerate((wl, wr)):
                eng.dma_start(w[:, l, i, :, :], m[bass.ds(e, 1), l, :, :].rearrange("e (c p) n -> p (e c) n", p=P)
                              ).then_inc(w_in[l], 16)
            eng.dma_start(bias[:, l, :], bl[bass.ds(e, 1), l, :].rearrange("e d -> (e d)")
                          .partition_broadcast(P)).then_inc(w_in[l], 16)

        with nc.Block() as block:
            @block.sync
            def _(sp):
                sp.dma_start(gw[:, :, :], gate_w.rearrange("(c p) e -> p c e", p=P)).then_inc(loaded, 16)
                sp.dma_start(gb[:, :], gate_b.partition_broadcast(P)).then_inc(loaded, 16)
                for l in range(LAYERS):
                    load_layer(sp, 0, l)
                with sp.Fori(0, GX - 1) as e:
                    for l in range(LAYERS):
                        sp.wait_ge(z_taken, e * 2 * TT + (2 + (l + 1) * TT))
                        load_layer(sp, e + 1, l)

            @block.gpsimd
            def _(pool):
                pool.iota(iota_i[:, :], pattern=[[1, GX]], base=0, channel_multiplier=0).then_inc(consts, 1)

            @block.vector
            def _(dve):
                step = Chain(dve, own)
                norm_rows(dve, step, st.x, st.xn, st.stats, st.mv, st.var[:, :], st.rstd[:, :], st.half[:, :],
                          st.tmp[:, :]).then_inc(xn_ready, 1)
                step(dve.tensor_scalar(inv[:, :], st.deg_in[:, :], 1.0, None, ALU.max))
                step(dve.reciprocal(inv[:, :], inv[:, :]))
                step(dve.scalar_tensor_tensor(inv[:, :], st.deg_in[:, :], 0.0, inv[:, :], ALU.is_gt, ALU.mult))
                for t in range(TT):
                    ins = dve.tensor_scalar(diag[:, t, :], st.ident[:, :], inv[:, t:t + 1], None, ALU.mult)
                ins.then_inc(diag_ready, 1)
                dve.wait_ge(consts, 1)
                step(dve.tensor_copy(iota[:, :], iota_i[:, :]))
                dve.wait_ge(inv_spread, 1)
                for q in range(2):
                    ins = dve.tensor_copy(inv_bc[:, q * 512:(q + 1) * 512], ps_z[:, q, :])
                step(ins)
                dve.wait_ge(scored, 1)
                step(dve.memset(prob[:, :, :], -1.0))
                step(dve.tensor_tensor(prob[:, :, 0:GX], ps_g[:, :, :],
                                       gb[:, :].unsqueeze(1).broadcast_to([P, TT, GX]), ALU.add))
                step(dve.tensor_reduce(peak[:, :], prob[:, :, 0:GX], AX.X, ALU.max))
                dve.tensor_tensor(prob[:, :, 0:GX], prob[:, :, 0:GX],
                                  peak[:, :].unsqueeze(2).broadcast_to([P, TT, GX]), ALU.subtract
                                  ).then_inc(logits, 1)
                dve.wait_ge(exp_done, 1)
                step(dve.tensor_reduce(peak[:, :], prob[:, :, 0:GX], AX.X, ALU.add))
                step(dve.reciprocal(peak[:, :], peak[:, :]))
                step(dve.tensor_tensor(prob[:, :, 0:GX], prob[:, :, 0:GX],
                                       peak[:, :].unsqueeze(2).broadcast_to([P, TT, GX]), ALU.mult))
                for t in range(TT):
                    ins = dve.max(best[:, t, :], prob[:, t, :])
                step(ins)
                for t in range(TT):
                    ins = dve.max_index(which[:, t, :], best[:, t, :], prob[:, t, :])
                step(ins)
                step(dve.tensor_copy(which_f[:, :, :], which[:, :, 0:TOPK]))
                for k in range(TOPK):
                    step(dve.tensor_tensor(pick[:, :, :], iota[:, :].unsqueeze(1).broadcast_to([P, TT, GX]),
                                           which_f[:, :, k].unsqueeze(2).broadcast_to([P, TT, GX]), ALU.is_equal))
                    if k == 0:
                        step(dve.tensor_tensor(gate[:, :, :], pick[:, :, :], prob[:, :, 0:GX], ALU.mult))
                    else:
                        step(dve.tensor_tensor(pick[:, :, :], pick[:, :, :], prob[:, :, 0:GX], ALU.mult))
                        step(dve.tensor_tensor(gate[:, :, :], gate[:, :, :], pick[:, :, :], ALU.add))

                def take_sums(out, start):
                    for i in range(2 * DC):
                        c, q = i // 2, i % 2
                        dve.wait_ge(sum_done, start + (i + 1))
                        dve.tensor_tensor(out[:, c, q * 512:(q + 1) * 512], ps_a[:, i % 2, :],
                                          inv_bc[:, q * 512:(q + 1) * 512], ALU.mult).then_inc(sum_taken, 1)

                dve.nop().then_inc(z_taken, 2)
                dve.nop().then_inc(sum_taken, 2)
                take_sums(meanT, 0)
                with dve.Fori(0, GX) as e:
                    step = LoopChain(dve, loop_own, e * OWN)
                    for l in range(LAYERS):
                        dve.wait_ge(w_in[l], (e + 1) * 48)
                        for t in range(TT):
                            u = l * TT + t
                            dve.wait_ge(z_done, e * 2 * TT + (u + 1))
                            dve.tensor_tensor(h[:, t, :], ps_z[:, t % 2, :], bias[:, l, :],
                                              ALU.add).then_inc(z_taken, 1)
                            if l == 1 and t >= 2:
                                dve.wait_ge(h_ready, e * 2 * TT + (u - 1))
                                step(dve.tensor_tensor(st.x[:, t - 2, :], st.x[:, t - 2, :], h[:, t - 2, :],
                                                       ALU.add))
                        if l == 0:
                            take_sums(mean2T, (e + 1) * 2 * DC)
                    for t in range(TT - 2, TT):
                        dve.wait_ge(h_ready, e * 2 * TT + (TT + t + 1))
                        step(dve.tensor_tensor(st.x[:, t, :], st.x[:, t, :], h[:, t, :], ALU.add))
                    assert step.n == OWN

            @block.tensor
            def _(pe):
                transpose_xn(pe, ps_t, st, xn_ready, xnT_ready, xnT_turned)
                pe.wait_ge(diag_ready, 1)
                for t in range(TT):
                    ins = pe.matmul(ps_z[:, t // 4, (t % 4) * P:(t % 4 + 1) * P], st.ones[:, :], diag[:, t, :],
                                    start=True, stop=True)
                ins.then_inc(inv_spread, 1)
                pe.wait_ge(loaded, 32)
                pe.wait_ge(xnT_ready, 2 * DC)
                for t in range(TT):
                    for c in range(DC):
                        ins = pe.matmul(ps_g[:, t, :], st.xnT[:, c, t * P:(t + 1) * P], gw[:, c, :],
                                        start=c == 0, stop=c == DC - 1)
                ins.then_inc(scored, 1)

                def sums(rows, start):
                    for i in range(2 * DC):
                        c, q = i // 2, i % 2
                        pe.wait_ge(sum_taken, start + (i + 1))
                        for s in range(TT):
                            ins = pe.matmul(ps_a[:, i % 2, :], rows[:, s, c * P:(c + 1) * P],
                                            st.countT[:, s, q * 512:(q + 1) * 512],
                                            start=s == 0, stop=s == TT - 1)
                        ins.then_inc(sum_done, 1)

                sums(st.xn, 0)
                with pe.Fori(0, GX) as e:
                    for l in range(LAYERS):
                        left, right = ((meanT, st.xnT), (mean2T, hT))[l]
                        for t in range(TT):
                            u = l * TT + t
                            if t == 0:
                                pe.wait_ge(w_in[l], (e + 1) * 48)
                                pe.wait_ge(sum_taken, (e + l) * 2 * DC + (2 + 2 * DC) if l else 2 + 2 * DC)
                                if l:
                                    pe.wait_ge(hT_taken, (e + 1) * 2 * DC + 2)
                            pe.wait_ge(z_taken, e * 2 * TT + (u + 1))
                            for i, m in enumerate((left, right)):
                                for c in range(DC):
                                    ins = pe.matmul(ps_z[:, t % 2, :], m[:, c, t * P:(t + 1) * P], w[:, l, i, c, :],
                                                    start=i == 0 and c == 0, stop=i == 1 and c == DC - 1)
                            ins.then_inc(z_done, 1)
                        if l == 0:
                            for i in range(2 * DC):
                                c, q = i // 2, i % 2
                                if i < 2:
                                    pe.wait_ge(h_ready, e * 2 * TT + 4 * (i + 1))
                                pe.wait_ge(hT_taken, e * 2 * DC + (i + 1))
                                for j in range(4):
                                    ins = pe.transpose(ps_t[:, i % 2, j * P:(j + 1) * P],
                                                       h[:, 4 * q + j, c * P:(c + 1) * P], st.ident[:, :])
                                ins.then_inc(h_turned, 1)
                            sums(h, (e + 1) * 2 * DC)

            @block.scalar
            def _(act):
                evacuate_xnT(act, ps_t, st, xnT_ready, xnT_turned)
                act.wait_ge(logits, 1)
                act.activation(prob[:, :, 0:GX], prob[:, :, 0:GX], ACT.Exp).then_inc(exp_done, 1)
                act.nop().then_inc(hT_taken, 2)
                with act.Fori(0, GX) as e:
                    for l in range(LAYERS):
                        for t in range(TT):
                            u = l * TT + t
                            act.wait_ge(z_taken, e * 2 * TT + (u + 3))
                            scale = gate[:, t, bass.ds(e, 1)] if l else 1.0
                            act.activation(h[:, t, :], h[:, t, :], ACT.Relu, scale=scale).then_inc(h_ready, 1)
                        if l == 0:
                            for i in range(2 * DC):
                                c, q = i // 2, i % 2
                                act.wait_ge(h_turned, e * 2 * DC + (i + 1))
                                act.activation(hT[:, c, q * 512:(q + 1) * 512], ps_t[:, i % 2, :],
                                               ACT.Copy).then_inc(hT_taken, 1)


TG, SE, SF = 16, 64, 32
NG = N // TG
GT = P // TG
QC = SE * SF // P
TIE = 1e-6


def stage_sets(kit, st, controller, f1, f2, out):
    nc = kit.nc
    with ExitStack() as ctx:
        sb = lambda *a: kit.sb(ctx, *a)
        sem = lambda n: kit.sem(ctx, n)
        ctl = sb("ctl", [P, DC, SE])
        f1_sb = sb("f1_sb", [P, DC, SE * SF])
        f2_sb = sb("f2_sb", [P, QC, D])
        big = sb("big", [P, QC, N])
        takenT = big[:, :, :].rearrange("p q n -> p (q n)").rearrange("p (c g s) -> p c g s", c=DC, s=SE)
        tie_i = sb("tie_i", [SE, TG], I32)
        tie = sb("tie", [SE, TG])
        logit = sb("logit", [SE, NG, TG])
        peak = sb("peak6", [SE, NG])
        maskT = sb("maskT", [SE, N])
        maskT_16 = sb("maskT_16", [SE, N], F16)
        mask = sb("mask6", [P, TT, SE])
        group = sb("group", [P, GT])
        block_mask = sb("block_mask", [P, 2, GT, SE])
        spread = sb("spread", [SE, QC, P], F16)
        hidden = sb("hidden", [P, QC, NG])
        ps_t = kit.ps(ctx, "ps_t6", [P, 2, 512])
        ps_l = kit.ps(ctx, "ps_l6", [SE, 2, 512])
        ps_a = kit.ps(ctx, "ps_a6", [P, 2, 512])
        ps_o = kit.ps(ctx, "ps_o", [P, 2, 512])

        loaded, f_in, consts, pool_own, own = sem("loaded6"), sem("f_in"), sem("consts6"), sem("pool_own6"), sem("own6")
        xn_ready, xnT_turned, xnT_ready = sem("xn_ready6"), sem("xnT_turned6"), sem("xnT_ready6")
        scored, mask_ready, mask_turned = sem("scored6"), sem("mask_ready"), sem("mask_turned")
        block_ready, taken_done, taken_ready = sem("block_ready"), sem("taken_done"), sem("taken_ready")
        hidden_done, hidden_ready = sem("hidden_done"), sem("hidden_ready")
        spread_done, spread_ready = sem("spread_done"), sem("spread_ready")
        out_done, out_ready, out_stored = sem("out_done"), sem("out_ready"), sem("out_stored")

        with nc.Block() as block:
            @block.sync
            def _(sp):
                sp.dma_start(ctl[:, :, :], controller.rearrange("(c p) e s -> p c (e s)", p=P)).then_inc(loaded, 16)
                sp.dma_start(f1_sb[:, :, :], f1.rearrange("(c p) e s f -> p c (e s f)", p=P)).then_inc(f_in, 16)
                sp.dma_start(f2_sb[:, :, :], f2.rearrange("e s f d -> (e s f) d").rearrange("(q p) d -> p q d", p=P)
                             ).then_inc(f_in, 16)
                for t in range(TT):
                    sp.wait_ge(out_ready, t + 1)
                    sp.dma_start(out[t * P:(t + 1) * P, :], st.x[:, t, :]).then_inc(out_stored, 16)
                sp.wait_ge(out_stored, TT * 16)

            @block.gpsimd
            def _(pool):
                step = Chain(pool, pool_own)
                pool.iota(tie_i[:, :], pattern=[[1, TG]], base=0, channel_multiplier=0)
                pool.memset(group[:, :], 1.0)
                step(pool.memset(spread[:, :, :], 1.0))
                step(pool.affine_select(out=group[:, :], in_=group[:, :], compare_op=ALU.is_ge, fill=0.0,
                                        base=0, pattern=[[-TG, GT]], channel_multiplier=1))
                step(pool.affine_select(out=group[:, :], in_=group[:, :], compare_op=ALU.is_ge, fill=0.0,
                                        base=TG - 1, pattern=[[TG, GT]], channel_multiplier=-1))
                step(pool.affine_select(out=spread[:, :, :], in_=spread[:, :, :], compare_op=ALU.is_ge, fill=0.0,
                                        base=0, pattern=[[P, QC], [1, P]], channel_multiplier=-SF))
                pool.affine_select(out=spread[:, :, :], in_=spread[:, :, :], compare_op=ALU.is_ge, fill=0.0,
                                   base=SF - 1, pattern=[[-P, QC], [-1, P]], channel_multiplier=SF
                                   ).then_inc(consts, 1)

            @block.vector
            def _(dve):
                step = Chain(dve, own)
                norm_rows(dve, step, st.x, st.xn, st.stats, st.mv, st.var[:, :], st.rstd[:, :], st.half[:, :],
                          st.tmp[:, :]).then_inc(xn_ready, 1)
                dve.wait_ge(consts, 1)
                step(dve.tensor_copy(tie[:, :], tie_i[:, :]))
                step(dve.tensor_scalar(tie[:, :], tie[:, :], TIE / (TG - 1), None, ALU.mult))
                dve.wait_ge(scored, 1)
                for q in range(2):
                    ins = dve.tensor_tensor(logit[:, q * NG // 2:(q + 1) * NG // 2, :],
                                            ps_l[:, q, :].rearrange("s (g t) -> s g t", t=TG),
                                            tie[:, :].unsqueeze(1).broadcast_to([SE, NG // 2, TG]), ALU.add)
                step(ins)
                step(dve.tensor_reduce(peak[:, :], logit[:, :, :], AX.X, ALU.max))
                dve.tensor_tensor(maskT[:, :].rearrange("s (g t) -> s g t", t=TG), logit[:, :, :],
                                  peak[:, :].unsqueeze(2).broadcast_to([SE, NG, TG]), ALU.is_equal
                                  ).then_inc(mask_ready, 1)
                dve.wait_ge(mask_ready, 1)
                dve.tensor_copy(maskT_16[:, :], maskT[:, :]).then_inc(mask_ready, 1)
                dve.wait_ge(mask_turned, 1)
                step(dve.tensor_copy(mask[:, :, :], ps_a[:, 0, :].rearrange("p (t s) -> p t s", s=SE)))
                for t in range(TT):
                    if t >= 2:
                        dve.wait_ge(taken_done, DC * (t - 1))
                    dve.tensor_tensor(block_mask[:, t % 2, :, :],
                                      mask[:, t, :].unsqueeze(1).broadcast_to([P, GT, SE]),
                                      group[:, :].unsqueeze(2).broadcast_to([P, GT, SE]), ALU.mult
                                      ).then_inc(block_ready, 1)
                dve.wait_ge(hidden_ready, QC)
                for i in range(2 * QC):
                    q, half = i // 2, i % 2
                    dve.wait_ge(spread_done, i + 1)
                    dve.tensor_tensor(big[:, q, half * 512:(half + 1) * 512].rearrange("p (g t) -> p g t", t=TG),
                                      ps_a[:, half, :].rearrange("p (g t) -> p g t", t=TG),
                                      hidden[:, q, half * NG // 2:(half + 1) * NG // 2].unsqueeze(2)
                                      .broadcast_to([P, NG // 2, TG]), ALU.mult).then_inc(spread_ready, 1)
                for t in range(TT):
                    dve.wait_ge(out_done, t + 1)
                    dve.tensor_tensor(st.x[:, t, :], st.x[:, t, :], ps_o[:, t % 2, :], ALU.add).then_inc(out_ready, 1)

            @block.tensor
            def _(pe):
                transpose_xn(pe, ps_t, st, xn_ready, xnT_ready, xnT_turned)
                pe.wait_ge(loaded, 16)
                pe.wait_ge(xnT_ready, 2 * DC)
                for q in range(2):
                    for c in range(DC):
                        ins = pe.matmul(ps_l[:, q, :], ctl[:, c, :], st.xnT[:, c, q * 512:(q + 1) * 512],
                                        start=c == 0, stop=c == DC - 1)
                ins.then_inc(scored, 1)
                pe.wait_ge(mask_ready, 1)
                for t in range(TT):
                    ins = pe.transpose(ps_a[:, 0, t * SE:(t + 1) * SE], maskT[:, t * P:(t + 1) * P],
                                       st.ident[0:SE, 0:SE])
                ins.then_inc(mask_turned, 1)
                for t in range(TT):
                    pe.wait_ge(block_ready, t + 1)
                    for c in range(DC):
                        u = t * DC + c
                        if u >= 2:
                            pe.wait_ge(taken_ready, u - 1)
                        pe.matmul(ps_t[:, u % 2, :], st.xn[:, t, c * P:(c + 1) * P],
                                  block_mask[:, t % 2, :, :].rearrange("p g s -> p (g s)"),
                                  start=True, stop=True).then_inc(taken_done, 1)
                pe.wait_ge(f_in, 32)
                pe.wait_ge(taken_ready, TT * DC)
                for q in range(QC):
                    if q >= 2:
                        pe.wait_ge(hidden_ready, q - 1)
                    for j in range(4):
                        s = 4 * q + j
                        for c in range(DC):
                            ins = pe.matmul(ps_o[j * SF:(j + 1) * SF, q % 2, 0:NG],
                                            f1_sb[:, c, s * SF:(s + 1) * SF], takenT[:, c, :, s],
                                            start=c == 0, stop=c == DC - 1, tile_position=(0, j * SF))
                    ins.then_inc(hidden_done, 1)
                pe.wait_ge(mask_ready, 2)
                pe.wait_ge(consts, 1)
                for i in range(2 * QC):
                    q, half = i // 2, i % 2
                    if i >= 2:
                        pe.wait_ge(spread_ready, i - 1)
                    pe.matmul(ps_a[:, half, :], spread[:, q, :], maskT_16[:, half * 512:(half + 1) * 512],
                              start=True, stop=True).then_inc(spread_done, 1)
                pe.wait_ge(spread_ready, 2 * QC)
                for t in range(TT):
                    if t >= 2:
                        pe.wait_ge(out_ready, t - 1)
                    for q in range(QC):
                        ins = pe.matmul(ps_o[:, t % 2, :], big[:, q, t * P:(t + 1) * P], f2_sb[:, q, :],
                                        start=q == 0, stop=q == QC - 1)
                    ins.then_inc(out_done, 1)

            @block.scalar
            def _(act):
                evacuate_xnT(act, ps_t, st, xnT_ready, xnT_turned)
                for t in range(TT):
                    for c in range(DC):
                        u = t * DC + c
                        act.wait_ge(taken_done, u + 1)
                        act.activation(takenT[:, c, t * GT:(t + 1) * GT, :],
                                       ps_t[:, u % 2, :].rearrange("p (g s) -> p g s", s=SE),
                                       ACT.Copy).then_inc(taken_ready, 1)
                for q in range(QC):
                    act.wait_ge(hidden_done, q + 1)
                    act.activation(hidden[:, q, :], ps_o[:, q % 2, 0:NG], ACT.Relu).then_inc(hidden_ready, 1)


def gnn_ffn_kernel(nc, x, src, dst, weights, out):
    kit = Kit(nc)
    with ExitStack() as ctx:
        with ExitStack() as graph_ctx:
            st = Persistent(kit, ctx, graph_ctx)
            stage_graph(kit, st, x, src, dst, *weights[0:2])
            stage_moe(kit, st, *weights[2:10])
            stage_sage(kit, st, *weights[10:15])
        stage_sets(kit, st, *weights[15:18], out)


_INS = ["x", "src", "dst", "L0_gnn_weight", "L0_gnn_bias", "L0_ffn_gate_w", "L0_ffn_gate_b", "L0_ffn_w1", "L0_ffn_b1",
        "L0_ffn_w2", "L0_ffn_b2", "L0_ffn_gamma", "L0_ffn_beta", "L1_gnn_gate_W", "L1_gnn_gate_b", "L1_gnn_Wl",
        "L1_gnn_bl", "L1_gnn_Wr", "L1_ffn_controller", "L1_ffn_f1", "L1_ffn_f2"]


def kernel(**inputs):
    import numpy as np
    import concourse.bacc as bacc
    from concourse.bass_utils import run_bass_kernel_spmd

    nc = bacc.Bacc("TRN2", target_bir_lowering=False, num_devices=1)
    arrays, args = {}, []
    for name in _INS:
        a = np.ascontiguousarray(inputs[name])
        arrays[f"in_{name}"] = a
        args.append(nc.dram_tensor(f"in_{name}", a.shape, mybir.dt.from_np(a.dtype), kind="ExternalInput").ap())
    out = nc.dram_tensor("out_0", (N, D), F32, kind="ExternalOutput").ap()
    gnn_ffn_kernel(nc, args[0], args[1], args[2], args[3:], out)
    results = run_bass_kernel_spmd(nc, [arrays], core_ids=[0])
    return results.results[0]["out_0"]
```

```python
from contextlib import ExitStack

import concourse.bass as bass
import concourse.mybir as mybir

P = 128
ALU = mybir.AluOpType
ACT = mybir.ActivationFunctionType
AX = mybir.AxisListType
F32 = mybir.dt.float32
F16 = mybir.dt.float16
FR = mybir.dt.float32r
I32 = mybir.dt.int32

N, D = 1024, 512
TT, DC = N // P, D // P
LN_EPS = 1e-5


class Chain:

    def __init__(self, sem):
        self.eng, self.sem, self.n = None, sem, 0

    def on(self, eng):
        self.eng = eng
        return self

    def __call__(self, ins):
        self.n += 1
        ins.then_inc(self.sem, 1)
        self.eng.wait_ge(self.sem, self.n)


class Kit:

    def __init__(self, nc, ctx):
        self.nc = nc
        self.semaphores = set()
        self.dve_chain = Chain(self.sem(ctx, "dve_own"))
        self.pool_chain = Chain(self.sem(ctx, "pool_own"))

    def sb(self, ctx, name, shape, dt=F32):
        return ctx.enter_context(self.nc.sbuf_tensor(name, shape, dt))

    def ps(self, ctx, name, shape, dt=F32):
        return ctx.enter_context(self.nc.psum_tensor(name, shape, dt))

    def sem(self, ctx, name):
        handle = ctx.enter_context(self.nc.semaphore(name))
        assert handle.num not in self.semaphores
        self.semaphores.add(handle.num)
        return handle


def rsqrt_steps(dve, step, out, var, eps, half, tmp):
    step(dve.tensor_scalar(half, var, eps, None, ALU.add))
    dve.tensor_scalar(tmp.bitcast(I32), half.bitcast(I32), 1, None, ALU.logical_shift_right)
    step(dve.tensor_scalar(half, half, -0.5, None, ALU.mult))
    step(dve.tensor_scalar(out.bitcast(I32), tmp.bitcast(I32), -1.0, float(0x5F3759DF), ALU.mult, ALU.add))
    for _ in range(3):
        if len(out.shape) == 2 and out.shape[1] == 1:
            step(dve.tensor_scalar(tmp, out, out, half, ALU.mult, ALU.mult))
        else:
            step(dve.tensor_tensor(tmp, out, out, ALU.mult))
            step(dve.tensor_tensor(tmp, tmp, half, ALU.mult))
        step(dve.scalar_tensor_tensor(out, tmp, 1.5, out, ALU.add, ALU.mult))


def row_stats(dve, st, t):
    return dve.bn_stats(st.stats[:, t, :], st.x[:, t, :])


def norm_stats(dve, step, st):
    for t in range(TT):
        ins = dve.bn_aggr(st.mv[:, t, :], st.stats[:, t, :])
    step(ins)
    step(dve.tensor_copy(st.var[:, :], st.mv[:, :, 1]))
    rsqrt_steps(dve, step, st.rstd[:, :], st.var[:, :], LN_EPS, st.half[:, :], st.tmp[:, :])


def norm_tile(dve, st, xn, t):
    return dve.tensor_scalar(xn[:, t, :], st.x[:, t, :], st.mv[:, t, 0:1], st.rstd[:, t:t + 1],
                             ALU.subtract, ALU.mult)


def product(pe, ps, left, right, n, start, stop, **kw):
    terms = [(a, b, i) for i in range(n) for a, b in ((0, 0), (0, 1), (1, 0))]
    for u, (a, b, i) in enumerate(terms):
        ins = pe.matmul(ps, left(a, i), right(b, i), start=start and u == 0, stop=stop and u == len(terms) - 1, **kw)
    return ins


E = 17408
EC = E // P
G = 4
ECP = EC + G
GROUPS = -(-EC // G)
COUNT_MAX = 4095


class Persistent:

    def __init__(self, kit, ctx, graph_ctx):
        sb = lambda *a: kit.sb(ctx, *a)
        self.x = sb("x", [P, TT, D])
        self.ident = sb("ident", [P, P])
        self.ones = sb("ones", [P, P])
        self.stats = sb("stats", [P, TT, 6])
        self.mv = sb("mv", [P, TT, 2])
        self.var = sb("var", [P, TT])
        self.rstd = sb("rstd", [P, TT])
        self.half = sb("half", [P, TT])
        self.tmp = sb("tmp", [P, TT])
        self.deg_in = kit.sb(graph_ctx, "deg_in", [P, TT])
        self.countT = kit.sb(graph_ctx, "countT", [P, TT, N], FR)
        self.many = kit.sb(graph_ctx, "many", [1, 1], I32)
        self.rest_dram = kit.nc.dram_tensor("rest_dram", (P, TT, N), F32, kind="Internal").ap()


def turn_tile(pe, ps, st, t, xn_ready, xnT_ready, xnT_turned):
    pe.wait_ge(xn_ready, t + 1)
    if t >= 2:
        pe.wait_ge(xnT_ready, t - 1)
    for c in range(DC):
        ins = pe.transpose(ps[:, t % 2, c * P:(c + 1) * P], st.xn[:, t, c * P:(c + 1) * P], st.ident[:, :])
    ins.then_inc(xnT_turned, 1)


def take_tile(act, ps, st, t, xnT_ready, xnT_turned):
    act.wait_ge(xnT_turned, t + 1)
    act.activation(st.xnT[:, :, t * P:(t + 1) * P], ps[:, t % 2, :].rearrange("p (c m) -> p c m", m=P), ACT.Copy
                   ).then_inc(xnT_ready, 1)


def stage_graph(kit, st, x, src, dst, weight, bias):
    nc = kit.nc
    with ExitStack() as ctx:
        sb = lambda *a: kit.sb(ctx, *a)
        sem = lambda n: kit.sem(ctx, n)
        with ExitStack() as early:
            st.xn = kit.sb(early, "xn", [P, TT, D])
            st.xnT = kit.sb(early, "xnT", [P, DC, N])
        h_hl = sb("h_hl", [P, 2, TT, D], FR)
        count = sb("count", [P, TT, N])
        adj = sb("adj", [P, TT, N], FR)
        wgt = sb("wgt", [P, DC, D])
        bias_bc = sb("bias_bc", [P, D])
        h = sb("h", [P, TT, D])
        rows_i = sb("rows_i", [P, 2, P], I32)
        tail_i = sb("tail_i", [EC - P, 2, P], I32)
        rows_f = sb("rows_f", [P, 2, P])
        tail_f = sb("tail_f", [EC - P, 2, P])
        ends = sb("ends", [P, 2, ECP])
        ends_local = sb("ends_local", [P, 2, ECP])
        lowhigh = sb("lowhigh", [P, 2, 2])
        diag = sb("diag", [P, 2, 2, P])
        spans = sb("spans", [TT, 2, EC])
        iota_i = sb("iota_i", [P, N], I32)
        iota_f = sb("iota_f", [P, EC])
        iota_16 = sb("iota_16", [P, N], F16)
        zero_16 = sb("zero_16", [P, P], F16)
        limit_i = sb("limit_i", [P, 2], I32)
        limit = sb("limit", [P, 2])
        shift_i = sb("shift_i", [P, TT], I32)
        shift = sb("shift", [P, TT])
        touch = sb("touch", [TT, EC])
        pick = sb("pick", [TT, EC])
        lohi = sb("lohi", [TT, 4])
        table_f = sb("table_f", [1, 4, TT])
        table = sb("table", [1, 4, TT], I32)
        hot_src = sb("hot_src", [P, G, N], F16)
        hot_dst = sb("hot_dst", [P, G, P], F16)
        deg = sb("deg", [P, TT])
        dinv = sb("dinv", [P, TT])
        ones_r = sb("ones_r", [P, 2], FR)
        over = sb("over", [P, TT])
        over_max = sb("over_max", [P, 1])
        rest = sb("rest0", [P, 2, 512])
        ps_c = kit.ps(ctx, "ps_c", [P, 2, N])
        ps_t = kit.ps(ctx, "ps_t", [P, 2, 512])
        ps_m = kit.ps(ctx, "ps_m", [P, 2, 512])

        edges_in, x_in, w_in = sem("edges_in"), sem("x_in"), sem("w_in")
        consts, localised = sem("consts"), sem("localised")
        rows_ready, rows_turned = sem("rows_ready"), sem("rows_turned")
        diag_ready, spans_there, lohi_ready = sem("diag_ready"), sem("spans_there"), sem("lohi_ready")
        table_moved, table_ready = sem("table_moved"), sem("table_ready")
        xn_ready, xnT_turned, xnT_ready = sem("xn_ready"), sem("xnT_turned"), sem("xnT_ready")
        h_done, h_ready = sem("h_done"), sem("h_ready")
        slots_free, slots_full = sem("slots_free"), sem("slots_full")
        tile_counted, count_taken, deg_summed = sem("tile_counted"), sem("count_taken"), sem("deg_summed")
        turned, turned_ready = sem("turned"), sem("turned_ready")
        adj_there = sem("adj_there")
        dinv_ready, high_ready, adj_ready = sem("dinv_ready"), sem("high_ready"), sem("adj_ready")
        over_ready, over_summed, many_ready = sem("over_ready"), sem("over_summed"), sem("many_ready")
        rest_turned, rest_ready, rest_stored = sem("rest_turned"), sem("rest_ready"), sem("rest_stored")
        mixed, mixed_free = sem("mixed"), sem("mixed_free")

        with nc.Block() as block:
            @block.sync
            def _(sp):
                for i, ends_dram in enumerate((src, dst)):
                    chunks = ends_dram.rearrange("(c e) -> c e", e=P)
                    sp.dma_start(rows_i[:, i, :], chunks[0:P, :]).then_inc(edges_in, 16)
                    sp.dma_start(tail_i[:, i, :], chunks[P:EC, :]).then_inc(edges_in, 16)
                sp.dma_start(st.x[:, :, :], x.rearrange("(t p) d -> p t d", p=P)).then_inc(x_in, 16)
                sp.dma_start(wgt[:, :, :], weight.rearrange("(c p) n -> p c n", p=P)).then_inc(w_in, 16)
                sp.dma_start(bias_bc[:, :], bias.partition_broadcast(P)).then_inc(w_in, 16)
                sp.wait_ge(lohi_ready, 1)
                for i in range(2):
                    sp.dma_start(table_f[0:1, i, :], lohi[:, i:i + 1]).then_inc(table_moved, 16)
                sp.wait_ge(table_moved, 32)
                sp.wait_ge(many_ready, 1)
                with sp.If(sp.value_load(st.many[0:1, 0:1], min_val=0, max_val=1)):
                    for i in range(2 * TT):
                        sp.wait_ge(rest_ready, i + 1)
                        sp.dma_start(st.rest_dram[:, i // 2, i % 2 * 512:(i % 2 + 1) * 512], rest[:, i % 2, :]
                                     ).then_inc(rest_stored, 16)
                        sp.wait_ge(rest_stored, (i + 1) * 16)

            @block.gpsimd
            def _(pool):
                step = kit.pool_chain.on(pool)
                step(pool.memset(st.ident[:, :], 0.0))
                step(pool.affine_select(out=st.ident[:, :], in_=st.ident[:, :], compare_op=ALU.not_equal, fill=1.0,
                                        base=0, pattern=[[-1, P]], channel_multiplier=1))
                pool.memset(st.ones[:, :], 1.0)
                pool.memset(zero_16[:, :], 0.0)
                pool.iota(iota_i[:, :], pattern=[[1, N]], base=0, channel_multiplier=0)
                pool.iota(limit_i[:, 0:1], pattern=[[0, 1]], base=0, channel_multiplier=P)
                pool.iota(limit_i[:, 1:2], pattern=[[0, 1]], base=P - 1, channel_multiplier=P)
                pool.memset(ends[:, :, EC:ECP], -1.0)
                pool.iota(shift_i[:, :], pattern=[[P, TT]], base=0, channel_multiplier=0).then_inc(consts, 1)

            @block.vector
            def _(dve):
                step = kit.dve_chain.on(dve)
                dve.wait_ge(consts, 1)
                dve.tensor_copy(iota_16[:, :], iota_i[:, :])
                dve.tensor_copy(iota_f[:, :], iota_i[:, 0:EC])
                dve.tensor_copy(limit[:, :], limit_i[:, :])
                dve.tensor_copy(ones_r[:, :], st.ones[:, 0:2])
                step(dve.tensor_copy(shift[:, :], shift_i[:, :]))
                dve.wait_ge(edges_in, 64)
                dve.tensor_copy(rows_f[:, :, :], rows_i[:, :, :])
                dve.tensor_copy(tail_f[:, :, :], tail_i[:, :, :]).then_inc(rows_ready, 1)
                dve.wait_ge(rows_ready, 1)
                for b, rows, n in ((0, rows_f, P), (1, tail_f, EC - P)):
                    for i, op in enumerate((ALU.min, ALU.max)):
                        ins = dve.tensor_reduce(lowhigh[0:n, b, i:i + 1], rows[:, 1, :], AX.X, op)
                step(ins)
                for b, n in ((0, P), (1, EC - P)):
                    for i in range(2):
                        ins = dve.tensor_scalar(diag[0:n, b, i, 0:n], st.ident[0:n, 0:n], lowhigh[0:n, b, i:i + 1],
                                                None, ALU.mult)
                ins.then_inc(diag_ready, 1)
                dve.wait_ge(rows_turned, 1)
                for i in range(2):
                    ins = dve.tensor_copy(ends[:, i, 0:EC], ps_t[:, i, 0:EC])
                step(ins)
                dve.wait_ge(spans_there, 1)
                step(dve.tensor_copy(spans[:, :, :], ps_m[0:TT, 0, 0:2 * EC].rearrange("m (i c) -> m i c", i=2)))
                step(dve.tensor_scalar(touch[:, :], spans[:, 0, :], limit[0:TT, 1:2], None, ALU.is_le))
                step(dve.scalar_tensor_tensor(touch[:, :], spans[:, 1, :], limit[0:TT, 0:1], touch[:, :],
                                              ALU.is_ge, ALU.mult))
                step(dve.tensor_tensor(pick[:, :], touch[:, :], iota_f[0:TT, :], ALU.mult))
                step(dve.tensor_reduce(lohi[:, 1:2], pick[:, :], AX.X, ALU.max))
                step(dve.scalar_tensor_tensor(pick[:, :], touch[:, :], -1000.0, iota_f[0:TT, :], ALU.mult, ALU.add))
                step(dve.tensor_reduce(lohi[:, 0:1], pick[:, :], AX.X, ALU.min))
                step(dve.tensor_scalar(lohi[:, 0:1], lohi[:, 0:1], 1000.0, lohi[:, 1:2], ALU.add, ALU.min))
                step(dve.tensor_scalar(lohi[:, 2:3], lohi[:, 1:2], lohi[:, 0:1], 1.0, ALU.subtract, ALU.add))
                step(dve.tensor_scalar(pick[:, 0:GROUPS], iota_f[0:TT, 0:EC:G], lohi[:, 2:3], None, ALU.is_lt))
                dve.tensor_reduce(lohi[:, 1:2], pick[:, 0:GROUPS], AX.X, ALU.add).then_inc(lohi_ready, 1)

                dve.wait_ge(x_in, 16)
                for t in range(TT):
                    ins = row_stats(dve, st, t)
                step(ins)
                norm_stats(dve, step, st)
                for t in range(TT):
                    norm_tile(dve, st, st.xn, t).then_inc(xn_ready, 1)

                dve.wait_ge(table_moved, 32)
                step(dve.tensor_tensor_scan(table_f[0:1, 3, :], st.ones[0:1, 0:TT], table_f[0:1, 1, :], 0.0,
                                            ALU.mult, ALU.add))
                step(dve.tensor_tensor(table_f[0:1, 2, :], table_f[0:1, 3, :], table_f[0:1, 1, :], ALU.subtract))
                dve.tensor_copy(table[0:1, :, :], table_f[0:1, :, :]).then_inc(table_ready, 1)
                dve.wait_ge(table_ready, 1)
                with dve.Fori(0, TT // 2) as pair:
                    spans_of = []
                    for b in range(2):
                        m = bass.ds(pair * 2 + b, 1)
                        spans_of.append((dve.value_load(table[0:1, 0, m], min_val=0, max_val=EC - 1),
                                         dve.value_load(table[0:1, 1, m], min_val=1, max_val=GROUPS),
                                         dve.value_load(table[0:1, 2, m], min_val=0, max_val=TT * GROUPS)))
                    for b, (first, groups, before) in enumerate(spans_of):
                        m = pair * 2 + b
                        dve.wait_ge(slots_free, before * G + 1)
                        dve.tensor_scalar(ends_local[:, b, :], ends[:, 1, :], shift[:, bass.ds(m, 1)], None,
                                          ALU.subtract).then_inc(localised, 1)
                        with dve.Fori(0, groups) as j:
                            chunk = (first + j * G).with_bounds(min_val=0, max_val=EC - 1)
                            for i in range(G):
                                dve.wait_ge(slots_free, (before + j) * G + (i + 1))
                                c = chunk + i
                                if i == 0:
                                    dve.wait_ge(localised, m + 1)
                                dve.tensor_scalar(hot_dst[:, i, :], iota_16[:, 0:P], ends_local[:, b, bass.ds(c, 1)],
                                                  None, ALU.is_equal)
                                dve.tensor_scalar(hot_src[:, i, :], iota_16[:, :], ends[:, 0, bass.ds(c, 1)],
                                                  None, ALU.is_equal).then_inc(slots_full, 1)

                dve.wait_ge(count_taken, TT)
                for t in range(TT):
                    own_block = adj[:, t, t * P:(t + 1) * P]
                    dve.wait_ge(turned_ready, 2 * t + 2)
                    step(dve.scalar_tensor_tensor(adj[:, t, :], count[:, t, :], 0.0, st.countT[:, t, :].bitcast(F32),
                                                  ALU.is_gt, ALU.max))
                    step(dve.tensor_scalar(adj[:, t, :], adj[:, t, :].bitcast(F32), 1.0, None, ALU.min))
                    dve.tensor_tensor(own_block, own_block.bitcast(F32), st.ident[:, :], ALU.add
                                      ).then_inc(adj_there, 1)
                for t in range(TT):
                    ins = dve.tensor_tensor(st.x[:, t, :], st.x[:, t, :], bias_bc[:, :], ALU.add)
                step(ins)
                dve.wait_ge(deg_summed, 1)
                step(dve.tensor_copy(deg[:, :], ps_c[:, 0, 0:2 * TT:2]))
                rsqrt_steps(dve, step, dinv[:, :], deg[:, :], 0.0, st.half[:, :], st.tmp[:, :])
                dve.nop().then_inc(dinv_ready, 1)
                dve.wait_ge(h_ready, TT)
                for t in range(TT):
                    dve.wait_ge(high_ready, t + 1)
                    dve.scalar_tensor_tensor(h_hl[:, 1, t, :], h[:, t, :], dinv[:, t:t + 1],
                                             h_hl[:, 0, t, :].bitcast(F32), ALU.mult, ALU.subtract
                                             ).then_inc(adj_ready, 1)
                for t in range(TT):
                    step(dve.tensor_reduce(st.deg_in[:, t:t + 1], count[:, t, :], AX.X, ALU.add))
                    dve.wait_ge(mixed, t + 1)
                    dve.scalar_tensor_tensor(st.x[:, t, :], ps_m[:, t % 2, :], dinv[:, t:t + 1], st.x[:, t, :],
                                             ALU.mult, ALU.add).then_inc(mixed_free, 1)
                    dve.wait_ge(mixed_free, t + 1)
                    row_stats(dve, st, t)
                step(dve.tensor_scalar(over[:, :], st.deg_in[:, :], float(COUNT_MAX), None, ALU.is_gt))
                dve.tensor_reduce(over_max[:, :], over[:, :], AX.X, ALU.max).then_inc(over_ready, 1)
                dve.wait_ge(over_summed, 1)
                dve.tensor_scalar(st.many[:, :], ps_c[0:1, 0, 0:1], 0.0, None, ALU.is_gt).then_inc(many_ready, 1)
                dve.wait_ge(many_ready, 1)
                with dve.If(dve.value_load(st.many[0:1, 0:1], min_val=0, max_val=1)):
                    for i in range(2 * TT):
                        dve.wait_ge(rest_turned, i + 1)
                        if i >= 2:
                            dve.wait_ge(rest_stored, (i - 1) * 16)
                        dve.tensor_tensor(rest[:, i % 2, :], ps_t[:, i % 2, :],
                                          st.countT[:, i // 2, i % 2 * 512:(i % 2 + 1) * 512].bitcast(F32),
                                          ALU.subtract).then_inc(rest_ready, 1)

            @block.tensor
            def _(pe):
                pe.wait_ge(rows_ready, 1)
                for i in range(2):
                    pe.transpose(ps_t[:, i, 0:P], rows_f[:, i, :], st.ident[:, :])
                    ins = pe.transpose(ps_t[:, i, P:EC], tail_f[:, i, :], st.ident[0:EC - P, 0:EC - P])
                ins.then_inc(rows_turned, 1)
                pe.wait_ge(diag_ready, 1)
                for i in range(2):
                    pe.matmul(ps_m[0:TT, 0, i * EC:i * EC + P], st.ones[:, 0:TT], diag[:, 0, i, :],
                              start=True, stop=True)
                    ins = pe.matmul(ps_m[0:TT, 0, i * EC + P:(i + 1) * EC], st.ones[0:EC - P, 0:TT],
                                    diag[0:EC - P, 1, i, 0:EC - P], start=True, stop=True)
                ins.then_inc(spans_there, 1)
                pe.wait_ge(w_in, 32)
                pe.wait_ge(lohi_ready, 1)
                for t in range(TT):
                    turn_tile(pe, ps_t, st, t, xn_ready, xnT_ready, xnT_turned)
                pe.nop().then_inc(slots_free, G)
                pe.wait_ge(table_ready, 1)
                for m in range(TT):
                    b = m % 2
                    groups = pe.value_load(table[0:1, 1, m:m + 1], min_val=1, max_val=GROUPS)
                    before = pe.value_load(table[0:1, 2, m:m + 1], min_val=0, max_val=TT * GROUPS)
                    if m >= 2:
                        pe.wait_ge(count_taken, m - 1)
                    for q in range(2):
                        pe.matmul(ps_c[:, b, q * 512:(q + 1) * 512], zero_16[:, :], iota_16[:, 0:512],
                                  start=True, stop=False, skip_group_check=True)
                    with pe.Fori(0, groups) as j:
                        for i in range(G):
                            pe.wait_ge(slots_full, (before + j) * G + (i + 1))
                            for q in range(2):
                                ins = pe.matmul(ps_c[:, b, q * 512:(q + 1) * 512], hot_dst[:, i, :],
                                                hot_src[:, i, q * 512:(q + 1) * 512],
                                                start=False, stop=False, skip_group_check=True)
                            ins.then_inc(slots_free, 1)
                    for q in range(2):
                        ins = pe.matmul(ps_c[:, b, q * 512:(q + 1) * 512], zero_16[:, :], iota_16[:, 0:512],
                                        start=False, stop=True, skip_group_check=True)
                    ins.then_inc(tile_counted, 1)
                    if m >= 2:
                        pe.wait_ge(h_ready, m - 1)
                    pe.wait_ge(xnT_ready, m + 1)
                    for c in range(DC):
                        ins = pe.matmul(ps_m[:, b, :], st.xnT[:, c, m * P:(m + 1) * P], wgt[:, c, :],
                                        start=c == 0, stop=c == DC - 1)
                    ins.then_inc(h_done, 1)
                def turn_counts(i):
                    s, half = i // 2, i % 2
                    for j in range(4):
                        ins = pe.transpose(ps_t[:, i % 2, j * P:(j + 1) * P],
                                           count[:, 4 * half + j, s * P:(s + 1) * P], st.ident[:, :])
                    return ins

                for i in range(2 * TT):
                    pe.wait_ge(count_taken, TT)
                    if i >= 2:
                        pe.wait_ge(turned_ready, i - 1)
                    turn_counts(i).then_inc(turned, 1)
                for s in range(TT):
                    pe.wait_ge(adj_there, s + 1)
                    for t in range(TT):
                        ins = pe.matmul(ps_c[:, 0, 2 * t:2 * t + 2], adj[:, s, t * P:(t + 1) * P], ones_r[:, :],
                                        start=s == 0 and t == 0, stop=s == TT - 1, skip_group_check=True)
                ins.then_inc(deg_summed, 1)
                for t in range(TT):
                    if t >= 2:
                        pe.wait_ge(mixed_free, t - 1)
                    for s in range(TT):
                        if t == 0:
                            pe.wait_ge(adj_ready, s + 1)
                        for part in range(2):
                            ins = pe.matmul(ps_m[:, t % 2, :], adj[:, s, t * P:(t + 1) * P], h_hl[:, part, s, :],
                                            start=s == 0 and part == 0, stop=s == TT - 1 and part == 1)
                    ins.then_inc(mixed, 1)
                pe.wait_ge(over_ready, 1)
                pe.matmul(ps_c[:, 0, 0:1], st.ones[:, :], over_max[:, :], start=True, stop=True
                          ).then_inc(over_summed, 1)
                pe.wait_ge(many_ready, 1)
                with pe.If(pe.value_load(st.many[0:1, 0:1], min_val=0, max_val=1)):
                    for i in range(2 * TT):
                        if i >= 2:
                            pe.wait_ge(rest_ready, i - 1)
                        turn_counts(i).then_inc(rest_turned, 1)

            @block.scalar
            def _(act):
                for t in range(TT):
                    take_tile(act, ps_t, st, t, xnT_ready, xnT_turned)
                for m in range(TT):
                    act.wait_ge(tile_counted, m + 1)
                    act.activation(count[:, m, :], ps_c[:, m % 2, :], ACT.Copy).then_inc(count_taken, 1)
                    act.wait_ge(h_done, m + 1)
                    act.activation(h[:, m, :], ps_m[:, m % 2, :], ACT.Copy).then_inc(h_ready, 1)
                for i in range(2 * TT):
                    s, half = i // 2, i % 2
                    act.wait_ge(turned, i + 1)
                    act.activation(st.countT[:, s, half * 512:(half + 1) * 512], ps_t[:, i % 2, :],
                                   ACT.Copy).then_inc(turned_ready, 1)
                act.wait_ge(dinv_ready, 1)
                for t in range(TT):
                    act.activation(h_hl[:, 0, t, :], h[:, t, :], ACT.Copy, scale=dinv[:, t:t + 1]
                                   ).then_inc(high_ready, 1)


EX, F, TOPK = 16, 1024, 2
FC = F // P
MAXT = N * TOPK // P + EX - 1
LISTS = 32
STEPS = 11
W2Q = 4


class LoopChain:

    def __init__(self, eng, sem, start):
        self.eng, self.sem, self.start, self.n = eng, sem, start, 0

    def __call__(self, ins):
        self.n += 1
        ins.then_inc(self.sem, 1)
        self.eng.wait_ge(self.sem, self.start + self.n)


def stage_moe(kit, st, gate_w, gate_b, w1, b1, w2, b2, gamma, beta):
    nc = kit.nc
    xn_dram = nc.dram_tensor("xn_dram", (N, D), F32, kind="Internal").ap()
    y_dram = nc.dram_tensor("y_dram", ((MAXT + 2) * P, D), F32, kind="Internal").ap()
    with ExitStack() as outer:
        weight = kit.sb(outer, "weight", [P, TT, TOPK])
        place = kit.sb(outer, "place", [P, TOPK, TT], mybir.dt.uint32)
        rowlist = kit.sb(outer, "rowlist", [P, LISTS + 2], mybir.dt.uint32)
        table = kit.sb(outer, "table_moe", [1, 2, EX], I32)
        first = kit.sb(outer, "first", [1, LISTS], I32)
        b1T = kit.sb(outer, "b1T", [P, EX * FC])
        w1_sb = kit.sb(outer, "w1_sb", [P, 2, DC, F])
        w2_sb = kit.sb(outer, "w2_sb", [P, FC, D])
        affine = kit.sb(outer, "affine", [P, 2, 3, D])
        w1_in = [kit.sem(outer, "w1_in0"), kit.sem(outer, "w1_in1")]
        w2_in = kit.sem(outer, "w2_in")
        affine_in = [kit.sem(outer, "affine_in0"), kit.sem(outer, "affine_in1")]
        xn_stored, listed_ready = kit.sem(outer, "xn_stored"), kit.sem(outer, "listed_ready")
        rows = kit.sb(outer, "rows", [P, D])
        rows_in = kit.sem(outer, "rows_in")

        def load_w1(sp, e, b):
            sp.dma_start(w1_sb[:, b, :, :], w1[bass.ds(e, 1)].rearrange("e (c p) f -> p (e c) f", p=P)
                         ).then_inc(w1_in[b], 16)
            for i, v in enumerate((b2, gamma, beta)):
                sp.dma_start(affine[:, b, i, :], v[bass.ds(e, 1)].rearrange("e d -> (e d)").partition_broadcast(P)
                             ).then_inc(affine_in[b], 16)

        def load_w2(sp, e):
            sp.dma_start(w2_sb[:, :, :], w2[bass.ds(e, 1)].rearrange("e (f p) d -> p (e f) d", p=P)
                         ).then_inc(w2_in, 16)

        with ExitStack() as ctx:
            sb = lambda *a: kit.sb(ctx, *a)
            sem = lambda n: kit.sem(ctx, n)
            st.xn = sb("xn3", [P, TT, D])
            st.xnT = sb("xnT3", [P, DC, N])
            gw = sb("gw", [P, DC, EX])
            gb = sb("gb", [P, EX])
            b1_rows = sb("b1_rows", [P, P])
            iota_i = sb("iota_i2", [P, P], I32)
            iota = sb("iota2", [P, P])
            node_i = sb("node_i", [P, TT], I32)
            node = sb("node", [P, TT])
            before = sb("before", [P, P])
            score = sb("score", [P, TT, EX])
            best = sb("best", [P, TT, 8])
            which = sb("which", [P, TT, 8], mybir.dt.uint32)
            which_f = sb("which_f", [P, TT, TOPK])
            hot = sb("hot", [P, TOPK, TT, EX])
            both = sb("both", [P, TT, EX])
            totals = sb("totals", [P, TT + 1, EX])
            rank = sb("rank", [P, TT, EX])
            tiles = sb("tiles", [P, EX])
            upto = sb("upto", [P, EX])
            start = sb("start", [P, EX])
            is_start = sb("is_start", [1, LISTS, EX - 1])
            first_f = sb("first_f", [1, LISTS])
            gap = sb("gap", [P, TT])
            ratio = sb("ratio", [P, TT])
            slot = sb("slot", [P, TOPK, TT])
            slot_i = sb("slot_i", [P, TOPK, TT], I32)
            part_i = sb("part_i", [P, 2, TOPK, TT], I32)
            part = sb("part", [P, 2, TOPK, TT])
            hot_row = sb("hot_row", [P, TOPK, TT, P], F16)
            hot_tile = sb("hot_tile", [P, TOPK, TT, LISTS], F16)
            ps_t = kit.ps(ctx, "ps_t2", [P, 2, 512])
            scoreT = sb("scoreT", [EX, N])
            ps_q = kit.ps(ctx, "ps_q", [EX, 2, 512])
            ps_s = kit.ps(ctx, "ps_s", [P, TT, EX])
            ps_r = kit.ps(ctx, "ps_r", [P, 512])
            ps_n = kit.ps(ctx, "ps_n", [P, 512])
            ps_l = kit.ps(ctx, "ps_l", [P, 512])

            consts, loaded = sem("consts3"), sem("loaded3")
            xn_ready, xnT_turned, xnT_ready = sem("xn_ready3"), sem("xnT_turned3"), sem("xnT_ready3")
            b1_turned, scored = sem("b1_turned"), sem("scored")
            scored_T, scoreT_ready = sem("scored_T"), sem("scoreT_ready")
            gap_ready, ratio_ready = sem("gap_ready"), sem("ratio_ready")
            both_ready, ranked = sem("both_ready"), sem("ranked")
            hots_ready, listed = sem("hots_ready"), sem("listed")

            with nc.Block() as block:
                @block.sync
                def _(sp):
                    sp.dma_start(gw[:, :, :], gate_w.rearrange("(c p) e -> p c e", p=P)).then_inc(loaded, 16)
                    sp.dma_start(gb[:, :], gate_b.partition_broadcast(P)).then_inc(loaded, 16)
                    sp.dma_start(b1_rows[:, :], b1.rearrange("e (f p) -> (e f) p", p=P)).then_inc(loaded, 16)
                    load_w1(sp, 0, 0)
                    load_w2(sp, 0)
                    sp.wait_ge(xn_ready, TT)
                    sp.dma_start(xn_dram.rearrange("(t p) d -> p t d", p=P), st.xn[:, :, :]).then_inc(xn_stored, 16)
                    load_w1(sp, 1, 1)
                    sp.wait_ge(xn_stored, 16)
                    for b in range(2):
                        sp.wait_ge(w1_in[b], 16)
                        sp.wait_ge(affine_in[b], 48)
                    sp.wait_ge(w2_in, 16)

                @block.gpsimd
                def _(pool):
                    step = kit.pool_chain.on(pool)
                    pool.iota(iota_i[:, :], pattern=[[1, P]], base=0, channel_multiplier=0)
                    pool.iota(node_i[:, :], pattern=[[P, TT]], base=0, channel_multiplier=1)
                    step(pool.memset(before[:, :], 1.0))
                    pool.affine_select(out=before[:, :], in_=before[:, :], compare_op=ALU.is_ge, fill=0.0,
                                       base=-1, pattern=[[1, P]], channel_multiplier=-1).then_inc(consts, 1)
                    pool.wait_ge(xn_stored, 16)
                    pool.wait_ge(listed_ready, 1)
                    pool.indirect_dma_start(out=rows[:, :], out_offset=None, in_=xn_dram,
                                            in_offset=bass.IndirectOffsetOnAxis(ap=rowlist[:, 0:1], axis=0)
                                            ).then_inc(rows_in, 16)

                @block.vector
                def _(dve):
                    step = kit.dve_chain.on(dve)
                    norm_stats(dve, step, st)
                    for t in range(TT):
                        norm_tile(dve, st, st.xn, t).then_inc(xn_ready, 1)
                    dve.wait_ge(consts, 1)
                    dve.tensor_copy(iota[:, :], iota_i[:, :])
                    step(dve.tensor_copy(node[:, :], node_i[:, :]))
                    dve.wait_ge(b1_turned, 1)
                    dve.tensor_copy(b1T[:, :], ps_l[:, 0:EX * FC])
                    dve.wait_ge(scored, 1)
                    step(dve.tensor_tensor(score[:, :, :], ps_s[:, :, :],
                                           gb[:, :].unsqueeze(1).broadcast_to([P, TT, EX]), ALU.add))
                    for t in range(TT):
                        ins = dve.max(best[:, t, :], score[:, t, :])
                    step(ins)
                    for t in range(TT):
                        dve.max_index(which[:, t, :], best[:, t, :], score[:, t, :])
                    dve.tensor_tensor(gap[:, :], best[:, :, 1], best[:, :, 0], ALU.subtract).then_inc(gap_ready, 1)
                    dve.wait_ge(gap_ready, 1)
                    step(dve.tensor_copy(which_f[:, :, :], which[:, :, 0:TOPK]))
                    for k in range(TOPK):
                        ins = dve.tensor_tensor(hot[:, k, :, :],
                                                iota[:, 0:EX].unsqueeze(1).broadcast_to([P, TT, EX]),
                                                which_f[:, :, k].unsqueeze(2).broadcast_to([P, TT, EX]),
                                                ALU.is_equal)
                    step(ins)
                    dve.tensor_tensor(both[:, :, :], hot[:, 0, :, :], hot[:, 1, :, :], ALU.add).then_inc(both_ready, 1)
                    dve.wait_ge(ratio_ready, 1)
                    step(dve.tensor_scalar(gap[:, :], ratio[:, :], 1.0, None, ALU.add))
                    step(dve.reciprocal(gap[:, :], gap[:, :]))
                    dve.tensor_copy(weight[:, :, 0], gap[:, :])
                    dve.tensor_tensor(weight[:, :, 1], gap[:, :], ratio[:, :], ALU.mult)
                    dve.wait_ge(ranked, 1)
                    step(dve.memset(totals[:, 0, :], 0.0))
                    for t in range(TT):
                        step(dve.tensor_tensor(totals[:, t + 1, :], totals[:, t, :], ps_n[:, t * EX:(t + 1) * EX],
                                               ALU.add))
                    dve.tensor_tensor(rank[:, :, :], totals[:, 0:TT, :],
                                      ps_r[:, 0:TT * EX].rearrange("p (t e) -> p t e", e=EX), ALU.add)
                    step(dve.memset(tiles[:, :], 1.0))
                    for k in range(1, TT):
                        step(dve.scalar_tensor_tensor(tiles[:, :], totals[:, TT, :], float(k * P), tiles[:, :],
                                                      ALU.is_gt, ALU.add))
                    step(dve.tensor_tensor_scan(upto[:, :], st.ones[:, 0:EX], tiles[:, :], 0.0, ALU.mult, ALU.add))
                    step(dve.tensor_tensor(start[:, :], upto[:, :], tiles[:, :], ALU.subtract))
                    dve.tensor_copy(table[0:1, 0, :], tiles[0:1, :])
                    dve.tensor_copy(table[0:1, 1, :], start[0:1, :])
                    step(dve.scalar_tensor_tensor(rank[:, :, :], start[:, :].unsqueeze(1).broadcast_to([P, TT, EX]),
                                                  float(P), rank[:, :, :], ALU.mult, ALU.add))
                    for k in range(TOPK):
                        ins = dve.tensor_tensor(hot[:, k, :, :], hot[:, k, :, :], rank[:, :, :], ALU.mult)
                    step(ins)
                    step(dve.tensor_reduce(slot[:, :, :], hot[:, :, :, :], AX.X, ALU.add))
                    step(dve.tensor_copy(slot_i[:, :, :], slot[:, :, :]))
                    dve.tensor_scalar(part_i[:, 0, :, :], slot_i[:, :, :], P - 1, None, ALU.bitwise_and)
                    dve.tensor_scalar(part_i[:, 1, :, :], slot_i[:, :, :], 7, None, ALU.logical_shift_right)
                    step(dve.tensor_scalar(place[:, :, :], slot[:, :, :], float(P), None, ALU.add))
                    step(dve.tensor_copy(part[:, :, :, :], part_i[:, :, :, :]))
                    for k in range(TOPK):
                        for t in range(TT):
                            dve.tensor_scalar(hot_row[:, k, t, :], iota[:, :], part[:, 0, k, t:t + 1], None,
                                              ALU.is_equal)
                            ins = dve.tensor_scalar(hot_tile[:, k, t, :], iota[:, 0:LISTS], part[:, 1, k, t:t + 1],
                                                    node[:, t:t + 1], ALU.is_equal, ALU.mult)
                            ins.then_inc(hots_ready, 1)
                    step(dve.tensor_tensor(is_start[:, :, :], iota[0:1, 0:LISTS].unsqueeze(2)
                                           .broadcast_to([1, LISTS, EX - 1]),
                                           start[0:1, 0:EX - 1].unsqueeze(1).broadcast_to([1, LISTS, EX - 1]),
                                           ALU.is_equal))
                    step(dve.tensor_reduce(first_f[:, :], is_start[:, :, :], AX.X, ALU.add))
                    dve.tensor_copy(first[:, :], first_f[:, :])
                    dve.wait_ge(listed, 1)
                    dve.memset(rowlist[:, LISTS:], 0)
                    dve.tensor_copy(rowlist[:, 0:LISTS], ps_l[:, 256:256 + LISTS]).then_inc(listed_ready, 1)

                @block.tensor
                def _(pe):
                    pe.wait_ge(loaded, 48)
                    pe.transpose(ps_l[:, 0:P], b1_rows[:, :], st.ident[:, :]).then_inc(b1_turned, 1)
                    for q in range(2):
                        for t in range(q * TT // 2, (q + 1) * TT // 2):
                            turn_tile(pe, ps_t, st, t, xn_ready, xnT_ready, xnT_turned)
                        pe.wait_ge(xnT_ready, (q + 1) * TT // 2)
                        for c in range(DC):
                            ins = pe.matmul(ps_q[:, q, :], gw[:, c, :], st.xnT[:, c, q * 512:(q + 1) * 512],
                                            start=c == 0, stop=c == DC - 1)
                        ins.then_inc(scored_T, 1)
                    for t in range(TT):
                        pe.wait_ge(scoreT_ready, t // (TT // 2) + 1)
                        ins = pe.transpose(ps_s[:, t, :], scoreT[:, t * P:(t + 1) * P], st.ident[0:EX, 0:EX])
                    ins.then_inc(scored, 1)
                    pe.wait_ge(both_ready, 1)
                    pe.wait_ge(consts, 1)
                    flat = both[:, :, :].rearrange("p t e -> p (t e)")
                    pe.matmul(ps_r[:, 0:TT * EX], before[:, :], flat, start=True, stop=True)
                    pe.matmul(ps_n[:, 0:TT * EX], st.ones[:, :], flat, start=True, stop=True).then_inc(ranked, 1)
                    for k in range(TOPK):
                        for t in range(TT):
                            pe.wait_ge(hots_ready, k * TT + t + 1)
                            ins = pe.matmul(ps_l[:, 256:256 + LISTS], hot_row[:, k, t, :], hot_tile[:, k, t, :],
                                            start=k == 0 and t == 0, stop=k == TOPK - 1 and t == TT - 1)
                    ins.then_inc(listed, 1)

                @block.scalar
                def _(act):
                    for t in range(TT):
                        take_tile(act, ps_t, st, t, xnT_ready, xnT_turned)
                    for q in range(2):
                        act.wait_ge(scored_T, q + 1)
                        act.activation(scoreT[:, q * 512:(q + 1) * 512], ps_q[:, q, :], ACT.Copy
                                       ).then_inc(scoreT_ready, 1)
                    act.wait_ge(gap_ready, 1)
                    act.activation(ratio[:, :], gap[:, :], ACT.Exp).then_inc(ratio_ready, 1)

        with ExitStack() as ctx:
            sb = lambda *a: kit.sb(ctx, *a)
            sem = lambda n: kit.sem(ctx, n)
            w2_hl = sb("w2_hl", [P, 2, 2, FC, D], FR)
            index = sb("index", [P, 1], mybir.dt.uint32)
            rowsT = sb("rowsT", [P, DC, P])
            hT = sb("hT", [P, FC, P])
            hT_hl = sb("hT_hl", [P, 2, FC, P], FR)
            y = sb("y", [P, D])
            y_norm = sb("y_norm", [P, D])
            y_out = sb("y_out", [P, D])
            zeros = sb("zeros", [P, D])
            stat = sb("stat", [P, 6])
            mean = sb("mean", [P, 2])
            rs = sb("rs", [P, 3])
            ps_x = kit.ps(ctx, "ps_x", [P, DC, P])
            ps_h = kit.ps(ctx, "ps_h", [P, FC, P])
            ps_y = kit.ps(ctx, "ps_y", [P, D])

            index_ready = sem("index_ready")
            w2_high, w2_ready = sem("w2_high"), sem("w2_ready")
            rows_turned, rowsT_ready = sem("rows_turned3"), sem("rowsT_ready")
            h_done, h_taken, h_high, hT_ready = sem("h_done3"), sem("h_taken"), sem("h_high"), sem("hT_ready")
            y_done, y_taken = sem("y_done"), sem("y_taken")
            y_normed, y_scaled = sem("y_normed"), sem("y_scaled")
            y_ready, y_stored = sem("y_ready"), sem("y_stored")
            own = sem("own3")
            zeros_ready, zeros_stored = sem("zeros_ready"), sem("zeros_stored")

            def expert(eng, pair, b):
                e = pair * 2 + b
                tiles = eng.value_load(table[0:1, 0, bass.ds(e, 1)], min_val=1, max_val=TT)
                before = eng.value_load(table[0:1, 1, bass.ds(e, 1)], min_val=0, max_val=MAXT - 1)
                return e, tiles, before

            with nc.Block() as block:
                @block.sync
                def _(sp):
                    sp.wait_ge(w2_ready, W2Q)
                    load_w2(sp, 1)
                    with sp.Fori(0, EX // 2 - 1) as pair:
                        for b in range(2):
                            e, tiles, before = expert(sp, pair, b)
                            sp.wait_ge(w2_ready, (e + 2) * W2Q)
                            load_w2(sp, e + 2)
                            sp.wait_ge(y_ready, before + tiles + 1)
                            load_w1(sp, e + 2, b)
                    _, n, before = expert(sp, EX // 2 - 1, 1)
                    sp.wait_ge(zeros_ready, 1)
                    with sp.Fori(0, before * -1 - n + (MAXT + 1)) as i:
                        tile = (before + n + 1 + i).with_bounds(min_val=0, max_val=MAXT + 1)
                        sp.dma_start(y_dram[bass.ds(tile * P, P), :], zeros[:, :]).then_inc(zeros_stored, 16)
                        sp.wait_ge(zeros_stored, (i + 1) * 16)

                @block.gpsimd
                def _(pool):
                    def gather():
                        pool.indirect_dma_start(out=rows[:, :], out_offset=None, in_=xn_dram,
                                                in_offset=bass.IndirectOffsetOnAxis(ap=index[:, :], axis=0)
                                                ).then_inc(rows_in, 16)

                    def gather_and_scale(g, pair, b):
                        pool.wait_ge(rows_turned, g + 2)
                        following = (g + 2).with_bounds(min_val=0, max_val=LISTS + 1)
                        pool.tensor_copy(index[:, :], rowlist[:, bass.ds(following, 1)]).then_inc(index_ready, 1)
                        pool.wait_ge(index_ready, 1)
                        pool.wait_ge(index_ready, g + 2)
                        gather()
                        pool.wait_ge(affine_in[b], (pair + 1) * 48)
                        pool.wait_ge(y_normed, g + 1)
                        pool.wait_ge(y_stored, (g + 1) * 16)
                        pool.tensor_tensor(y_out[:, :], y_norm[:, :], affine[:, b, 1, :], ALU.mult
                                           ).then_inc(y_scaled, 1)
                        pool.wait_ge(y_scaled, g + 1)
                        pool.tensor_tensor(y_out[:, :], y_out[:, :], affine[:, b, 2, :], ALU.add
                                           ).then_inc(y_ready, 1)
                        pool.wait_ge(y_ready, g + 2)

                    pool.wait_ge(rows_turned, 1)
                    pool.tensor_copy(index[:, :], rowlist[:, 1:2]).then_inc(index_ready, 1)
                    pool.wait_ge(index_ready, 1)
                    gather()
                    pool.memset(y_out[:, :], 0.0).then_inc(y_ready, 1)
                    with pool.Fori(0, EX // 2) as pair:
                        for b in range(2):
                            _, tiles, before = expert(pool, pair, b)
                            with pool.Fori(0, tiles) as j:
                                gather_and_scale(before + j, pair, b)
                    last = pool.value_load(table[0:1, 1, EX - 1:EX], min_val=0, max_val=MAXT - 1)
                    n = pool.value_load(table[0:1, 0, EX - 1:EX], min_val=1, max_val=TT)
                    pool.wait_ge(rows_in, (last + n + 2) * 16)
                    pool.tensor_tensor(y_norm[:, 0:1], affine[:, 1, 1, 0:1], affine[:, 1, 1, 0:1], ALU.mult)
                @block.tensor
                def _(pe):
                    def turn(g):
                        pe.wait_ge(rows_in, (g + 1) * 16)
                        for c in range(DC):
                            ins = pe.transpose(ps_x[:, c, :], rows[:, c * P:(c + 1) * P], st.ident[:, :])
                        ins.then_inc(rows_turned, 1)
                    turn(0)
                    with pe.Fori(0, EX // 2) as pair:
                        for b in range(2):
                            _, tiles, before = expert(pe, pair, b)
                            with pe.Fori(0, tiles) as j:
                                g = before + j
                                pe.wait_ge(w1_in[b], (pair + 1) * 16)
                                pe.wait_ge(rowsT_ready, g + 1)
                                for f in range(FC):
                                    if f % 4 == 0:
                                        pe.wait_ge(h_taken, (g + 1) * 2 + (f // 4 - 1))
                                    for c in range(DC):
                                        ins = pe.matmul(ps_h[:, f, :], w1_sb[:, b, c, f * P:(f + 1) * P],
                                                        rowsT[:, c, :], start=c == 0, stop=c == DC - 1)
                                    if f % 4 == 3:
                                        ins.then_inc(h_done, 1)
                                turn(g + 1)
                                pe.wait_ge(w2_ready, (pair * 2 + (b + 1)) * W2Q)
                                pe.wait_ge(y_taken, g + 1)
                                for i in range(2):
                                    pe.wait_ge(hT_ready, g * 2 + (i + 1))
                                    ins = product(pe, ps_y[:, :], lambda a, f: hT_hl[:, a, i * 4 + f, :],
                                                  lambda a, f: w2_hl[:, b, a, i * 4 + f, :], FC // 2,
                                                  i == 0, i == 1)
                                ins.then_inc(y_done, 1)

                @block.scalar
                def _(act):
                    def take_rows(g):
                        act.wait_ge(rows_turned, g + 1)
                        act.activation(rowsT[:, :, :], ps_x[:, :, :], ACT.Copy).then_inc(rowsT_ready, 1)

                    def store(g):
                        act.wait_ge(y_ready, g + 1)
                        act.dma_start(y_dram[bass.ds(g * P, P), :], y_out[:, :]).then_inc(y_stored, 16)
                    def split_w2(number, b):
                        act.wait_ge(w2_in, number * 16)
                        for i in range(W2Q):
                            part = slice(i * FC // W2Q, (i + 1) * FC // W2Q)
                            act.activation(w2_hl[:, b, 0, part, :], w2_sb[:, part, :], ACT.Copy).then_inc(w2_high, 1)

                    act.nop().then_inc(h_taken, 2)
                    take_rows(0)
                    split_w2(1, 0)
                    with act.Fori(0, EX // 2) as pair:
                        for b in range(2):
                            e, tiles, before = expert(act, pair, b)
                            with act.Fori(0, tiles) as j:
                                g = (before + j).with_bounds(min_val=0, max_val=MAXT - 1)
                                for f in range(FC):
                                    if f % 4 == 0:
                                        act.wait_ge(h_done, g * 2 + (f // 4 + 1))
                                        act.wait_ge(y_done, g + 1)
                                    ins = act.activation(hT[:, f, :], ps_h[:, f, :], ACT.Gelu,
                                                         bias=b1T[:, bass.ds(e * FC + f, 1)])
                                    if f % 4 == 3:
                                        ins.then_inc(h_taken, 1)
                                        act.wait_ge(h_taken, g * 2 + (f // 4 + 3))
                                        act.activation(hT_hl[:, 0, f - 3:f + 1, :], hT[:, f - 3:f + 1, :], ACT.Copy
                                                       ).then_inc(h_high, 1)
                                take_rows(g + 1)
                                store(g)
                                with act.If(act.value_load(first[0:1, bass.ds(g, 1)], min_val=0, max_val=1)):
                                    split_w2(e + 2, 1 - b)
                    _, n, last = expert(act, EX // 2 - 1, 1)
                    store((last + n).with_bounds(min_val=1, max_val=MAXT))
                    act.wait_ge(y_stored, (last + n + 1) * 16)
                    act.activation(hT[:, 0, 0:1], hT[:, 0, 0:1], ACT.Copy)

                @block.vector
                def _(dve):
                    dve.memset(zeros[:, :], 0.0).then_inc(zeros_ready, 1)
                    def split_w2(number, b):
                        for i in range(W2Q):
                            part = slice(i * FC // W2Q, (i + 1) * FC // W2Q)
                            dve.wait_ge(w2_high, number * W2Q + (i + 1 - W2Q))
                            dve.tensor_tensor(w2_hl[:, b, 1, part, :], w2_sb[:, part, :],
                                              w2_hl[:, b, 0, part, :].bitcast(F32), ALU.subtract).then_inc(w2_ready, 1)

                    split_w2(1, 0)
                    dve.nop().then_inc(y_taken, 1)
                    dve.nop().then_inc(y_done, 1)
                    with dve.Fori(0, EX // 2) as pair:
                        for b in range(2):
                            e, tiles, before = expert(dve, pair, b)
                            with dve.Fori(0, tiles) as j:
                                g = (before + j).with_bounds(min_val=0, max_val=MAXT - 1)
                                for i in range(2):
                                    dve.wait_ge(h_high, g * 2 + (i + 1))
                                    half = slice(i * 4, i * 4 + 4)
                                    dve.tensor_tensor(hT_hl[:, 1, half, :], hT[:, half, :],
                                                      hT_hl[:, 0, half, :].bitcast(F32), ALU.subtract
                                                      ).then_inc(hT_ready, 1)
                                with dve.If(dve.value_load(first[0:1, bass.ds(g, 1)], min_val=0, max_val=1)):
                                    split_w2(e + 2, 1 - b)
                                step = LoopChain(dve, own, g * STEPS)
                                dve.wait_ge(affine_in[b], (pair + 1) * 48)
                                dve.wait_ge(y_done, g + 2)
                                ins = dve.tensor_tensor(y[:, :], ps_y[:, :], affine[:, b, 0, :], ALU.add)
                                ins.then_inc(y_taken, 1)
                                dve.wait_ge(y_taken, g + 2)
                                step(dve.bn_stats(stat[:, :], y[:, :]))
                                dve.memset(rs[:, 0:1], 0.0)
                                step(dve.bn_aggr(mean[:, :], stat[:, :]))
                                rsqrt_steps(dve, step, rs[:, 0:1], mean[:, 1:2], LN_EPS, rs[:, 1:2], rs[:, 2:3])
                                dve.wait_ge(y_ready, g + 1)
                                dve.tensor_scalar(y_norm[:, :], y[:, :], mean[:, 0:1], rs[:, 0:1],
                                                  ALU.subtract, ALU.mult).then_inc(y_normed, 1)
                                dve.wait_ge(y_normed, g + 1)
                                assert step.n == STEPS

        with ExitStack() as ctx:
            sem = lambda n: kit.sem(ctx, n)
            taken = kit.sb(ctx, "taken", [P, TOPK, TT, D])
            rows_in = [sem(f"rows_in4_{i}") for i in range(TT // 2)]
            with nc.Block() as block:
                @block.gpsimd
                def _(pool):
                    for t in range(TT):
                        for k in range(TOPK):
                            pool.indirect_dma_start(out=taken[:, k, t, :], out_offset=None, in_=y_dram,
                                                    in_offset=bass.IndirectOffsetOnAxis(
                                                        ap=place[:, k, t:t + 1], axis=0)).then_inc(rows_in[t // 2], 16)

                @block.vector
                def _(dve):
                    step = kit.dve_chain.on(dve)
                    for t in range(TT):
                        dve.wait_ge(rows_in[t // 2], 64)
                        for k in range(TOPK):
                            step(dve.scalar_tensor_tensor(st.x[:, t, :], taken[:, k, t, :], weight[:, t, k:k + 1],
                                                          st.x[:, t, :], ALU.mult, ALU.add))
                        row_stats(dve, st, t)


GX, LAYERS = 4, 2
HQ = 4


def sum_rows(pe, ps, st, rows, t, many, rest, rest_in, rest_used, number):
    for s in range(TT):
        if s == TT // 2:
            with pe.If(many):
                pe.wait_ge(rest_in, number * 16)
                for r in range(TT):
                    for part in range(2):
                        ins = pe.matmul(ps, rest[:, r, :], rows[:, part, r, :], start=False, stop=False,
                                        skip_group_check=True)
                ins.then_inc(rest_used, 1)
        for part in range(2):
            ins = pe.matmul(ps, st.countT[:, s, t * P:(t + 1) * P], rows[:, part, s, :],
                            start=s == 0 and part == 0, stop=s == TT - 1 and part == 1, skip_group_check=True)
    return ins


def load_rest(pool, st, rest, rest_in, rest_used, tiles, steps):
    many = pool.value_load(st.many[0:1, 0:1], min_val=0, max_val=1)
    with pool.If(many):
        with pool.Fori(0, steps) as step:
            with pool.Fori(0, tiles) as t:
                pool.wait_ge(rest_used, step * tiles + t + 1)
                pool.dma_start(rest[:, :, :].bitcast(F32), st.rest_dram[:, :, bass.ds(t * P, P)]).then_inc(rest_in, 16)
                pool.wait_ge(rest_in, (step * tiles + t + 1) * 16)


def stage_sage(kit, st, gate_w, gate_b, wl, bl, wr):
    nc = kit.nc
    hT_dram = nc.dram_tensor("hT_dram", (GX, 2, D, N), F32, kind="Internal").ap()
    with ExitStack() as outer:
        gate = kit.sb(outer, "gate", [P, TT, GX])
        inv = kit.sb(outer, "inv", [P, TT])
        bias = kit.sb(outer, "bias5", [P, GX * LAYERS * DC])
        rest = kit.sb(outer, "rest", [P, TT, P], FR)
        prob = kit.sb(outer, "prob", [P, TT, 8])
        w = kit.sb(outer, "w52", [P, 2, DC, D])
        w_in = kit.sem(outer, "w_in52")
        with ExitStack() as inputs:
            xnT = kit.sb(inputs, "xnT5", [P, 2, DC, N], FR)
            meanT = kit.sb(inputs, "meanT", [P, 2, DC, N], FR)
            sage_inputs(kit, st, gate_w, gate_b, bl, prob, inv, bias, rest, xnT, meanT)
            sage_first_layers(kit, st, wl, wr, prob, gate, bias, xnT, meanT, w, w_in, hT_dram)
        sage_second_layers(kit, st, wl, wr, bl, gate, inv, rest, w, w_in, hT_dram)


def load_second(sp, w, w_in, wl, wr, e):
    for i, m in enumerate((wl, wr)):
        sp.dma_start(w[:, i, :, :], m[bass.ds(e, 1), 1, :, :].rearrange("e (c p) n -> p (e c) n", p=P)
                     ).then_inc(w_in, 16)


def sage_inputs(kit, st, gate_w, gate_b, bl, prob, inv, bias, rest, xnT, meanT):
    nc = kit.nc
    with ExitStack() as ctx:
        sb = lambda *a: kit.sb(ctx, *a)
        sem = lambda n: kit.sem(ctx, n)
        xn = sb("xn5", [P, TT, D])
        xn_hl = sb("xn_hl", [P, 2, TT, D], FR)
        mean = sb("mean5", [P, 2, D])
        gw = sb("gw5", [P, DC, GX])
        gw_hl = sb("gw_hl5", [P, 2, DC, GX], FR)
        gb = sb("gb5", [P, GX])
        bias_rows = sb("bias_rows5", [GX * LAYERS * DC, P])
        ps_t = kit.ps(ctx, "ps_t5", [P, 2, DC, P])
        ps_a = kit.ps(ctx, "ps_a5", [P, 2, D])
        ps_g = kit.ps(ctx, "ps_g5", [P, TT, GX])
        ps_b = kit.ps(ctx, "ps_b5", [P, GX * LAYERS * DC])

        loaded = sem("loaded5")
        xn_ready, high_ready, low_ready = sem("xn_ready5"), sem("high_ready5"), sem("low_ready5")
        gw_high, gw_ready = sem("gw_high5"), sem("gw_ready5")
        turned, turned_high, turned_low = sem("turned5"), sem("turned_high5"), sem("turned_low5")
        bias_turned = sem("bias_turned5")
        scored = sem("scored5")
        sum_done, mean_ready = sem("sum_done5"), sem("mean_ready5")
        rest_in, rest_used = sem("rest_in5"), sem("rest_used5")

        with nc.Block() as block:
            @block.sync
            def _(sp):
                sp.dma_start(gw[:, :, :], gate_w.rearrange("(c p) e -> p c e", p=P)).then_inc(loaded, 16)
                sp.dma_start(gb[:, :], gate_b.partition_broadcast(P)).then_inc(loaded, 16)
                sp.dma_start(bias_rows[:, :], bl.rearrange("e l (c p) -> (e l c) p", p=P)).then_inc(loaded, 16)

            @block.gpsimd
            def _(pool):
                load_rest(pool, st, rest, rest_in, rest_used, TT, 1)

            @block.vector
            def _(dve):
                step = kit.dve_chain.on(dve)
                norm_stats(dve, step, st)
                for t in range(TT):
                    norm_tile(dve, st, xn, t).then_inc(xn_ready, 1)
                dve.wait_ge(loaded, 48)
                dve.wait_ge(gw_high, 1)
                dve.tensor_tensor(gw_hl[:, 1, :, :], gw[:, :, :], gw_hl[:, 0, :, :].bitcast(F32), ALU.subtract
                                  ).then_inc(gw_ready, 1)
                for t in range(TT):
                    dve.wait_ge(high_ready, t + 1)
                    dve.tensor_tensor(xn_hl[:, 1, t, :], xn[:, t, :], xn_hl[:, 0, t, :].bitcast(F32), ALU.subtract
                                      ).then_inc(low_ready, 1)
                    dve.wait_ge(turned_high, t + 1)
                    dve.tensor_tensor(xnT[:, 1, :, t * P:(t + 1) * P], ps_t[:, t % 2, :, :],
                                      xnT[:, 0, :, t * P:(t + 1) * P].bitcast(F32), ALU.subtract
                                      ).then_inc(turned_low, 1)
                step(dve.tensor_scalar(inv[:, :], st.deg_in[:, :], 1.0, None, ALU.max))
                step(dve.reciprocal(inv[:, :], inv[:, :]))
                step(dve.scalar_tensor_tensor(inv[:, :], st.deg_in[:, :], 0.0, inv[:, :], ALU.is_gt, ALU.mult))
                for t in range(TT + 1):
                    if t < TT:
                        dve.wait_ge(sum_done, t + 1)
                        if t >= 2:
                            dve.wait_ge(turned, TT + t - 1)
                        dve.tensor_scalar(mean[:, t % 2, :], ps_a[:, t % 2, :], inv[:, t:t + 1], None, ALU.mult
                                          ).then_inc(mean_ready, 1)
                    if t >= 1:
                        u = t - 1
                        dve.wait_ge(turned_high, TT + u + 1)
                        dve.tensor_tensor(meanT[:, 1, :, u * P:(u + 1) * P], ps_t[:, u % 2, :, :],
                                          meanT[:, 0, :, u * P:(u + 1) * P].bitcast(F32), ALU.subtract
                                          ).then_inc(turned_low, 1)
                dve.wait_ge(bias_turned, 1)
                dve.tensor_copy(bias[:, :], ps_b[:, :])
                dve.wait_ge(scored, 1)
                step(dve.memset(prob[:, :, :], -1.0))
                dve.tensor_tensor(prob[:, :, 0:GX], ps_g[:, :, :],
                                  gb[:, :].unsqueeze(1).broadcast_to([P, TT, GX]), ALU.add)

            @block.tensor
            def _(pe):
                many = pe.value_load(st.many[0:1, 0:1], min_val=0, max_val=1)
                pe.wait_ge(loaded, 48)
                n = GX * LAYERS * DC
                pe.transpose(ps_b[:, :], bias_rows[:, :], st.ident[0:n, 0:n]).then_inc(bias_turned, 1)
                for t in range(TT):
                    pe.wait_ge(xn_ready, t + 1)
                    if t >= 2:
                        pe.wait_ge(turned_low, t - 1)
                    for c in range(DC):
                        ins = pe.transpose(ps_t[:, t % 2, c, :], xn[:, t, c * P:(c + 1) * P], st.ident[:, :])
                    ins.then_inc(turned, 1)
                pe.wait_ge(gw_ready, 1)
                for t in range(TT):
                    pe.wait_ge(turned_low, t + 1)
                    ins = product(pe, ps_g[:, t, :], lambda a, c: xnT[:, a, c, t * P:(t + 1) * P],
                                  lambda b, c: gw_hl[:, b, c, :], DC, True, True)
                ins.then_inc(scored, 1)
                pe.wait_ge(low_ready, TT)
                pe.nop().then_inc(rest_used, 1)
                for t in range(TT + 1):
                    if t < TT:
                        if t >= 2:
                            pe.wait_ge(mean_ready, t - 1)
                        sum_rows(pe, ps_a[:, t % 2, :], st, xn_hl, t, many, rest, rest_in, rest_used, t + 1
                                 ).then_inc(sum_done, 1)
                    if t >= 1:
                        u = t - 1
                        pe.wait_ge(mean_ready, u + 1)
                        pe.wait_ge(turned_low, TT + u - 1)
                        for c in range(DC):
                            ins = pe.transpose(ps_t[:, u % 2, c, :], mean[:, u % 2, c * P:(c + 1) * P],
                                               st.ident[:, :])
                        ins.then_inc(turned, 1)

            @block.scalar
            def _(act):
                for t in range(TT):
                    act.wait_ge(xn_ready, t + 1)
                    act.activation(xn_hl[:, 0, t, :], xn[:, t, :], ACT.Copy).then_inc(high_ready, 1)
                    act.wait_ge(turned, t + 1)
                    act.activation(xnT[:, 0, :, t * P:(t + 1) * P], ps_t[:, t % 2, :, :], ACT.Copy
                                   ).then_inc(turned_high, 1)
                    if t == 0:
                        act.wait_ge(loaded, 48)
                        act.activation(gw_hl[:, 0, :, :], gw[:, :, :], ACT.Copy).then_inc(gw_high, 1)
                for t in range(TT):
                    act.wait_ge(turned, TT + t + 1)
                    act.activation(meanT[:, 0, :, t * P:(t + 1) * P], ps_t[:, t % 2, :, :], ACT.Copy
                                   ).then_inc(turned_high, 1)


def sage_first_layers(kit, st, wl, wr, prob, gate, bias, xnT, meanT, w2, w2_in, hT_dram):
    nc = kit.nc
    PAIRS = GX // 2
    UNITS = [(b, j) for b in range(2) for j in range(DC)]

    def over_pairs(eng, body):
        with eng.Fori(0, PAIRS - 1) as pair:
            body(pair, False)
        body(PAIRS - 1, True)

    with ExitStack() as ctx:
        sb = lambda *a: kit.sb(ctx, *a)
        sem = lambda n: kit.sem(ctx, n)
        w = sb("w51", [P, 2, 2, DC, D])
        w_hl = sb("w_hl51", [P, 2, 2, 2, DC, P], FR)
        h = sb("h51", [P, 2, 512])
        h_hl = sb("h_hl51", [P, 2, 2, N], FR)
        bias_now = sb("bias_now", [P, 2 * LAYERS * DC])
        iota_i = sb("iota_i5", [P, GX], I32)
        iota = sb("iota5", [P, GX])
        best = sb("best5", [P, TT, 8])
        which = sb("which5", [P, TT, 8], mybir.dt.uint32)
        which_f = sb("which_f5", [P, TT, TOPK])
        pick = sb("pick5", [P, TT, GX])
        peak = sb("peak", [P, TT])
        ps = kit.ps(ctx, "ps51", [P, 4, 512])
        w_in = [sem("w_in51_0"), sem("w_in51_1")]
        w_high, w_ready = sem("w_high51"), sem("w_ready51")
        done, relued, high, low = sem("done51"), sem("relued51"), sem("high51"), sem("low51")
        stored = [sem("stored51_0"), sem("stored51_1")]
        bias_moved, consts = sem("bias_moved"), sem("consts51")
        logits, exp_done = sem("logits5"), sem("exp_done5")

        with nc.Block() as block:
            @block.sync
            def _(sp):
                def load(e, b):
                    for i, m in enumerate((wl, wr)):
                        sp.dma_start(w[:, b, i, :, :], m[bass.ds(e, 1), 0, :, :].rearrange("e (c p) n -> p (e c) n", p=P)
                                     ).then_inc(w_in[b], 16)

                def store(pair, b, j):
                    u = (pair * 2 + b) * DC + j
                    sp.wait_ge(low, u * 2 + 4)
                    sp.dma_start(hT_dram[bass.ds(pair * 2 + b, 1), :, j * P:(j + 1) * P, :]
                                 .rearrange("e a p n -> p (e a) n"), h_hl[:, j % 2, :, :].bitcast(F32)
                                 ).then_inc(stored[j % 2], 16)

                for b in range(2):
                    load(b, b)
                for j in range(DC):
                    store(0, 0, j)
                with sp.Fori(0, PAIRS - 1) as pair:
                    for b in range(2):
                        sp.wait_ge(w_ready, (pair * 2 + (b + 1)) * DC)
                        load(pair * 2 + (b + 2), b)
                        for j in range(DC):
                            store(pair + b, 1 - b, j)
                load_second(sp, w2, w2_in, wl, wr, 0)
                for j in range(DC):
                    store(PAIRS - 1, 1, j)
                for slot in range(2):
                    sp.wait_ge(stored[slot], (GX * DC // 2 + 1) * 16)
                sp.wait_ge(w2_in, 32)

            @block.gpsimd
            def _(pool):
                pool.iota(iota_i[:, :], pattern=[[1, GX]], base=0, channel_multiplier=0).then_inc(consts, 1)

            @block.scalar
            def _(act):
                def split_w(pair, b, j):
                    if j == 0:
                        act.wait_ge(w_in[b], (pair + 1) * 32)
                    act.wait_ge(done, ((pair * 2 + b) * DC + j) * 2 + 1)
                    act.activation(w_hl[:, j % 2, 0, :, :, :].rearrange("p i c m -> p (i c) m"),
                                   w[:, b, :, :, j * P:(j + 1) * P].rearrange("p i c m -> p (i c) m"),
                                   ACT.Copy).then_inc(w_high, 1)

                def relu(pair, b, j):
                    u = (pair * 2 + b) * DC + j
                    for q in range(2):
                        v = u * 2 + q
                        act.wait_ge(done, v + 4)
                        act.wait_ge(low, v + 1)
                        act.activation(h[:, q, :], ps[:, (2 * j + q) % 4, :], ACT.Relu,
                                       bias=bias_now[:, b * LAYERS * DC + j:b * LAYERS * DC + j + 1]
                                       ).then_inc(relued, 1)
                        act.wait_ge(relued, v + 5)
                        act.wait_ge(stored[j % 2], ((pair * 2 + b) * (DC // 2) + (j // 2 + 1)) * 16)
                        act.activation(h_hl[:, j % 2, 0, q * 512:(q + 1) * 512], h[:, q, :], ACT.Copy
                                       ).then_inc(high, 1)

                def body(pair, last):
                    act.activation(bias_now[:, :], bias[:, bass.ds(pair * (2 * LAYERS * DC), 2 * LAYERS * DC)],
                                   ACT.Copy).then_inc(bias_moved, 1)
                    act.wait_ge(bias_moved, pair + 1)
                    for b, j in UNITS:
                        if (b, j) != UNITS[-1]:
                            split_w(pair, *UNITS[b * DC + j + 1])
                        elif not last:
                            split_w(pair + 1, 0, 0)
                        if last and b == 1 and j == 0:
                            act.wait_ge(logits, 1)
                            act.activation(prob[:, :, 0:GX], prob[:, :, 0:GX], ACT.Exp).then_inc(exp_done, 1)
                        relu(pair, b, j)

                for slot in range(2):
                    act.nop().then_inc(stored[slot], 16)
                split_w(0, 0, 0)
                over_pairs(act, body)

            @block.vector
            def _(dve):
                def split_w(u, b, j):
                    dve.wait_ge(w_high, u + 1)
                    dve.tensor_tensor(w_hl[:, j % 2, 1, :, :, :].rearrange("p i c m -> p (i c) m"),
                                      w[:, b, :, :, j * P:(j + 1) * P].rearrange("p i c m -> p (i c) m"),
                                      w_hl[:, j % 2, 0, :, :, :].rearrange("p i c m -> p (i c) m")
                                      .bitcast(F32), ALU.subtract).then_inc(w_ready, 1)

                def softmax(step):
                    step(dve.tensor_copy(iota[:, :], iota_i[:, :]))
                    step(dve.tensor_reduce(peak[:, :], prob[:, :, 0:GX], AX.X, ALU.max))
                    dve.tensor_tensor(prob[:, :, 0:GX], prob[:, :, 0:GX],
                                      peak[:, :].unsqueeze(2).broadcast_to([P, TT, GX]), ALU.subtract
                                      ).then_inc(logits, 1)

                def choose(step):
                    step(dve.tensor_reduce(peak[:, :], prob[:, :, 0:GX], AX.X, ALU.add))
                    step(dve.reciprocal(peak[:, :], peak[:, :]))
                    step(dve.tensor_tensor(prob[:, :, 0:GX], prob[:, :, 0:GX],
                                           peak[:, :].unsqueeze(2).broadcast_to([P, TT, GX]), ALU.mult))
                    for t in range(TT):
                        ins = dve.max(best[:, t, :], prob[:, t, :])
                    step(ins)
                    for t in range(TT):
                        ins = dve.max_index(which[:, t, :], best[:, t, :], prob[:, t, :])
                    step(ins)
                    step(dve.tensor_copy(which_f[:, :, :], which[:, :, 0:TOPK]))
                    for k in range(TOPK):
                        step(dve.tensor_tensor(pick[:, :, :], iota[:, :].unsqueeze(1).broadcast_to([P, TT, GX]),
                                               which_f[:, :, k].unsqueeze(2).broadcast_to([P, TT, GX]),
                                               ALU.is_equal))
                        if k == 0:
                            step(dve.tensor_tensor(gate[:, :, :], pick[:, :, :], prob[:, :, 0:GX], ALU.mult))
                        else:
                            step(dve.tensor_tensor(pick[:, :, :], pick[:, :, :], prob[:, :, 0:GX], ALU.mult))
                            step(dve.tensor_tensor(gate[:, :, :], gate[:, :, :], pick[:, :, :], ALU.add))

                def body(pair, last):
                    for b, j in UNITS:
                        u = (pair * 2 + b) * DC + j
                        if (b, j) != UNITS[-1]:
                            split_w(u + 1, *UNITS[b * DC + j + 1])
                        elif not last:
                            split_w(u + 1, 0, 0)
                        for q in range(2):
                            dve.wait_ge(high, u * 2 + (q + 1))
                            half = h_hl[:, j % 2, :, q * 512:(q + 1) * 512]
                            dve.tensor_tensor(half[:, 1, :], h[:, q, :], half[:, 0, :].bitcast(F32),
                                              ALU.subtract).then_inc(low, 1)
                        if last and b == 0 and j == 2:
                            dve.wait_ge(consts, 1)
                            softmax(step)
                        if last and b == 1 and j == 1:
                            dve.wait_ge(exp_done, 1)
                            choose(step)

                step = kit.dve_chain.on(dve)
                dve.nop().then_inc(low, 2)
                split_w(0, 0, 0)
                over_pairs(dve, body)

            @block.tensor
            def _(pe):
                pe.nop().then_inc(done, 3)
                pe.nop().then_inc(relued, 4)

                def body(pair, last):
                    for b, j in UNITS:
                        u = (pair * 2 + b) * DC + j
                        pe.wait_ge(w_ready, u + 1)
                        for q in range(2):
                            pe.wait_ge(relued, u * 2 + (q + 1))
                            product(pe, ps[:, (2 * j + q) % 4, :],
                                    lambda a, i: w_hl[:, j % 2, a, i // DC, i % DC, :],
                                    lambda a, i: (meanT, xnT)[i // DC][:, a, i % DC, q * 512:(q + 1) * 512],
                                    2 * DC, True, True).then_inc(done, 1)
                over_pairs(pe, body)


def sage_second_layers(kit, st, wl, wr, bl, gate, inv, rest, w, w_in, hT_dram):
    nc = kit.nc
    with ExitStack() as ctx:
        sb = lambda *a: kit.sb(ctx, *a)
        sem = lambda n: kit.sem(ctx, n)
        hT = sb("hT52", [P, 2, DC, N], FR)
        hw = sb("hw52", [P, 2, TT, D], FR)
        w_hl = sb("w_hl52", [P, 2, 2, DC, D], FR)
        bias = sb("bias52", [P, 1, D])
        z = sb("z52", [P, 2, D])
        ps_w = kit.ps(ctx, "ps_w52", [P, 2, D])
        ps_a = kit.ps(ctx, "ps_a52", [P, 2, D])
        ps_r = kit.ps(ctx, "ps_r52", [P, 2, D])

        bias_in, h_in = sem("bias_in52"), [sem(f"h_in52_{q}") for q in range(HQ)]
        w_high, w_ready = sem("w_high52"), sem("w_ready52")
        hw_done, hw_high, hw_ready = sem("hw_done"), sem("hw_high"), sem("hw_ready")
        z_done, r_taken, z_ready, relued = sem("z_done52"), sem("r_taken52"), sem("z_ready52"), sem("relued52")
        rest_in, rest_used, own = sem("rest_in52"), sem("rest_used52"), sem("own52")

        def over_experts(eng, body):
            with eng.Fori(0, GX - 1) as e:
                body(e, False)
            body(GX - 1, True)

        with nc.Block() as block:
            @block.sync
            def _(sp):
                def load_bias(e, b):
                    sp.dma_start(bias[:, b, :], bl[bass.ds(e, 1), 1, :].rearrange("e d -> (e d)")
                                 .partition_broadcast(P)).then_inc(bias_in, 16)

                def load_h(e, q):
                    for a in range(2):
                        sp.dma_start(hT[:, a, :, q * N // HQ:(q + 1) * N // HQ].bitcast(F32),
                                     hT_dram[bass.ds(e, 1), a, :, q * N // HQ:(q + 1) * N // HQ]
                                     .rearrange("e (c p) n -> p (e c) n", p=P)).then_inc(h_in[q], 16)

                for q in range(HQ):
                    load_h(0, q)
                load_bias(0, 0)
                with sp.Fori(0, GX - 1) as e:
                    sp.wait_ge(w_ready, e * 2 + 2)
                    load_second(sp, w, w_in, wl, wr, e + 1)
                    for q in range(HQ):
                        sp.wait_ge(r_taken, e * TT + (TT // HQ * (q + 1) + 2))
                        load_h(e + 1, q)
                    sp.wait_ge(z_ready, e * TT + TT)
                    load_bias(e + 1, 0)

            @block.gpsimd
            def _(pool):
                load_rest(pool, st, rest, rest_in, rest_used, TT, GX)

            @block.scalar
            def _(act):
                def split_w(number, i):
                    act.wait_ge(w_in, number)
                    act.activation(w_hl[:, i, 0, :, :], w[:, i, :, :], ACT.Copy).then_inc(w_high, 1)

                split_w(32, 0)

                def body(e, last):
                    for t in range(TT):
                        act.wait_ge(hw_done, e * TT + (t + 1))
                        act.activation(hw[:, 0, t, :], ps_w[:, t % 2, :], ACT.Copy).then_inc(hw_high, 1)
                        if t == 0:
                            split_w((e + 1) * 32, 1)
                    for t in range(TT):
                        act.wait_ge(z_ready, e * TT + (t + 1))
                        column = e if last else e.with_bounds(min_val=0, max_val=GX - 1)
                        act.activation(z[:, t % 2, :], z[:, t % 2, :], ACT.Relu, scale=gate[:, t, bass.ds(column, 1)]
                                       ).then_inc(relued, 1)
                        if t == 1 and not last:
                            split_w((e + 2) * 32, 0)
                over_experts(act, body)

            @block.vector
            def _(dve):
                def split_w(number, i):
                    dve.wait_ge(w_high, number)
                    dve.tensor_tensor(w_hl[:, i, 1, :, :], w[:, i, :, :], w_hl[:, i, 0, :, :].bitcast(F32),
                                      ALU.subtract).then_inc(w_ready, 1)

                split_w(1, 0)
                dve.nop().then_inc(r_taken, 2)

                def body(e, last):
                    step = LoopChain(dve, own, e * (2 * TT))

                    def add(t):
                        dve.wait_ge(relued, e * TT + (t + 1))
                        step(dve.tensor_tensor(st.x[:, t, :], st.x[:, t, :], z[:, t % 2, :], ALU.add))
                        if last:
                            row_stats(dve, st, t)

                    for t in range(TT):
                        dve.wait_ge(hw_high, e * TT + (t + 1))
                        dve.tensor_tensor(hw[:, 1, t, :], ps_w[:, t % 2, :], hw[:, 0, t, :].bitcast(F32),
                                          ALU.subtract).then_inc(hw_ready, 1)
                        if t == 0:
                            split_w(e * 2 + 2, 1)
                    for t in range(TT):
                        if t == 0:
                            dve.wait_ge(bias_in, (e + 1) * 16)
                        dve.wait_ge(z_done, e * TT + (t + 1))
                        step(dve.tensor_tensor(z[:, t % 2, :], ps_r[:, t % 2, :], bias[:, 0, :], ALU.add))
                        dve.scalar_tensor_tensor(z[:, t % 2, :], ps_a[:, t % 2, :], inv[:, t:t + 1], z[:, t % 2, :],
                                                 ALU.mult, ALU.add).then_inc(z_ready, 1)
                        dve.wait_ge(z_ready, e * TT + (t + 1))
                        dve.nop().then_inc(r_taken, 1)
                        if t >= 1:
                            add(t - 1)
                        if t == 1 and not last:
                            split_w(e * 2 + 3, 0)
                    add(TT - 1)
                    assert step.n == 2 * TT
                over_experts(dve, body)

            @block.tensor
            def _(pe):
                many = pe.value_load(st.many[0:1, 0:1], min_val=0, max_val=1)
                pe.nop().then_inc(rest_used, 1)
                pe.nop().then_inc(hw_ready, 2)

                def body(e, last):
                    left = lambda t: lambda a, c: hT[:, a, c, t * P:(t + 1) * P]
                    for t in range(TT):
                        if t == 0:
                            pe.wait_ge(w_ready, e * 2 + 1)
                        if t % (TT // HQ) == 0:
                            pe.wait_ge(h_in[t // (TT // HQ)], e * 32 + 32)
                        pe.wait_ge(hw_ready, e * TT + (t + 1))
                        product(pe, ps_w[:, t % 2, :], left(t), lambda a, c: w_hl[:, 0, a, c, :], DC, True, True
                                ).then_inc(hw_done, 1)
                    for t in range(TT):
                        if t == 0:
                            pe.wait_ge(hw_ready, e * TT + (TT + 2))
                            pe.wait_ge(w_ready, e * 2 + 2)
                        pe.wait_ge(r_taken, e * TT + (t + 1))
                        sum_rows(pe, ps_a[:, t % 2, :], st, hw, t, many, rest, rest_in, rest_used,
                                 e * TT + (t + 1))
                        product(pe, ps_r[:, t % 2, :], left(t), lambda a, c: w_hl[:, 1, a, c, :], DC, True, True
                                ).then_inc(z_done, 1)
                over_experts(pe, body)


TG, SE, SF = 16, 64, 32
NG = N // TG
GT = P // TG
QC = SE * SF // P
TIE = 1e-6
F2Q = 2


def stage_sets(kit, st, controller, f1, f2, out):
    nc = kit.nc
    with ExitStack() as ctx:
        sb = lambda *a: kit.sb(ctx, *a)
        sem = lambda n: kit.sem(ctx, n)
        tie_i = sb("tie_i", [SE, TG], I32)
        tie = sb("tie", [SE, TG])
        peak = sb("peak6", [SE, NG])
        maskT_16 = sb("maskT_16", [SE, N], F16)
        mask = sb("mask6", [P, TT, SE])
        group = sb("group", [P, GT])
        block_mask = sb("block_mask", [P, 2, GT, SE], FR)
        spread = sb("spread", [SE, QC, P], F16)
        hidden = sb("hidden", [P, QC, NG])
        ctl = sb("ctl", [P, DC, SE])
        f1_sb = sb("f1_sb", [P, DC, SE * SF])
        with ExitStack() as early:
            st.xnT = kit.sb(early, "xnT6", [P, DC, N])
            logit = kit.sb(early, "logit", [SE, NG, TG])
            maskT = kit.sb(early, "maskT", [SE, N])
            st.xn = kit.sb(early, "xn6", [P, TT, D])
            xn_hl = kit.sb(early, "xn_hl6", [P, 2, TT, D], FR)
        f2_raw = sb("f2_raw", [P, 2, F2Q, D])
        f2_hl = sb("f2_hl", [P, 2, QC, D], FR)
        with ExitStack() as early:
            takenT = kit.sb(early, "takenT", [P, DC, NG, SE])
        big = sb("big", [P, 2, QC, P])
        big_hl = sb("big_hl", [P, 2, 2, QC, P], FR)
        ps_w = kit.ps(ctx, "ps_w6", [P, 4, 512])
        ps_t, ps_l = ps_w[:, 0:2, :], ps_w[0:SE, 2:4, :]
        ps_a = kit.ps(ctx, "ps_a6", [P, 512])
        ps_o = kit.ps(ctx, "ps_o", [P, 2, 512])

        loaded, f_in, consts = sem("loaded6"), sem("f_in"), sem("consts6")
        xn_ready, xnT_turned, xnT_ready = sem("xn_ready6"), sem("xnT_turned6"), sem("xnT_ready6")
        high_ready, low_ready = sem("high_ready6"), sem("low_ready6")
        f2_in, f2_high, f2_ready = [sem("f2_in0"), sem("f2_in1")], sem("f2_high"), sem("f2_ready")
        big_high, big_ready = sem("big_high"), sem("big_ready")
        scored, mask_ready, mask_turned = sem("scored6"), sem("mask_ready"), sem("mask_turned")
        block_ready, taken_done, taken_ready = sem("block_ready"), sem("taken_done"), sem("taken_ready")
        hidden_done, hidden_ready = sem("hidden_done"), sem("hidden_ready")
        spread_done, spread_ready = sem("spread_done"), sem("spread_ready")
        out_done, out_ready, out_stored = sem("out_done"), sem("out_ready"), sem("out_stored")

        with nc.Block() as block:
            @block.sync
            def _(sp):
                sp.dma_start(ctl[:, :, :], controller.rearrange("(c p) e s -> p c (e s)", p=P)).then_inc(loaded, 16)
                sp.dma_start(f1_sb[:, :, :], f1.rearrange("(c p) e s f -> p c (e s f)", p=P)).then_inc(f_in, 16)
                sp.wait_ge(scored, 1)
                for i in range(QC // F2Q):
                    if i >= 2:
                        sp.wait_ge(f2_ready, i - 1)
                    sp.dma_start(f2_raw[:, i % 2, :, :], f2.rearrange("e s f d -> (e s f) d")
                                 .rearrange("(q p) d -> p q d", p=P)[:, i * F2Q:(i + 1) * F2Q, :]
                                 ).then_inc(f2_in[i % 2], 16)
                for t in range(TT):
                    sp.wait_ge(out_ready, t + 1)
                    sp.dma_start(out[t * P:(t + 1) * P, :], st.x[:, t, :]).then_inc(out_stored, 16)
                sp.wait_ge(out_stored, TT * 16)

            @block.gpsimd
            def _(pool):
                step = kit.pool_chain.on(pool)
                pool.iota(tie_i[:, :], pattern=[[1, TG]], base=0, channel_multiplier=0)
                pool.memset(group[:, :], 1.0)
                step(pool.memset(spread[:, :, :], 1.0))
                step(pool.affine_select(out=group[:, :], in_=group[:, :], compare_op=ALU.is_ge, fill=0.0,
                                        base=0, pattern=[[-TG, GT]], channel_multiplier=1))
                step(pool.affine_select(out=group[:, :], in_=group[:, :], compare_op=ALU.is_ge, fill=0.0,
                                        base=TG - 1, pattern=[[TG, GT]], channel_multiplier=-1))
                step(pool.affine_select(out=spread[:, :, :], in_=spread[:, :, :], compare_op=ALU.is_ge, fill=0.0,
                                        base=0, pattern=[[P, QC], [1, P]], channel_multiplier=-SF))
                pool.affine_select(out=spread[:, :, :], in_=spread[:, :, :], compare_op=ALU.is_ge, fill=0.0,
                                   base=SF - 1, pattern=[[-P, QC], [-1, P]], channel_multiplier=SF
                                   ).then_inc(consts, 1)

            @block.vector
            def _(dve):
                step = kit.dve_chain.on(dve)
                norm_stats(dve, step, st)
                for t in range(TT):
                    norm_tile(dve, st, st.xn, t).then_inc(xn_ready, 1)
                dve.wait_ge(consts, 1)
                step(dve.tensor_copy(tie[:, :], tie_i[:, :]))
                step(dve.tensor_scalar(tie[:, :], tie[:, :], TIE / (TG - 1), None, ALU.mult))
                for t in range(TT):
                    dve.wait_ge(high_ready, t + 1)
                    dve.tensor_tensor(xn_hl[:, 1, t, :], st.xn[:, t, :], xn_hl[:, 0, t, :].bitcast(F32), ALU.subtract
                                      ).then_inc(low_ready, 1)
                dve.wait_ge(scored, 1)
                for q in range(2):
                    ins = dve.tensor_tensor(logit[:, q * NG // 2:(q + 1) * NG // 2, :],
                                            ps_l[:, q, :].rearrange("s (g t) -> s g t", t=TG),
                                            tie[:, :].unsqueeze(1).broadcast_to([SE, NG // 2, TG]), ALU.add)
                step(ins)
                step(dve.tensor_reduce(peak[:, :], logit[:, :, :], AX.X, ALU.max))
                dve.tensor_tensor(maskT[:, :].rearrange("s (g t) -> s g t", t=TG), logit[:, :, :],
                                  peak[:, :].unsqueeze(2).broadcast_to([SE, NG, TG]), ALU.is_equal
                                  ).then_inc(mask_ready, 1)
                dve.wait_ge(mask_ready, 1)
                dve.tensor_copy(maskT_16[:, :], maskT[:, :]).then_inc(mask_ready, 1)
                dve.wait_ge(mask_turned, 1)
                step(dve.tensor_copy(mask[:, :, :], ps_a[:, :].rearrange("p (t s) -> p t s", s=SE)))
                for t in range(TT):
                    if t >= 2:
                        dve.wait_ge(taken_done, DC * (t - 1))
                    dve.tensor_tensor(block_mask[:, t % 2, :, :],
                                      mask[:, t, :].unsqueeze(1).broadcast_to([P, GT, SE]),
                                      group[:, :].unsqueeze(2).broadcast_to([P, GT, SE]), ALU.mult
                                      ).then_inc(block_ready, 1)
                for i in range(QC // F2Q):
                    part = slice(i * F2Q, (i + 1) * F2Q)
                    dve.wait_ge(f2_high, i + 1)
                    dve.tensor_tensor(f2_hl[:, 1, part, :], f2_raw[:, i % 2, :, :],
                                      f2_hl[:, 0, part, :].bitcast(F32), ALU.subtract).then_inc(f2_ready, 1)
                dve.wait_ge(hidden_ready, QC)
                for t in range(TT + 1):
                    if t < TT:
                        for half in range(2):
                            i = 2 * t + half
                            qs = slice(half * QC // 2, (half + 1) * QC // 2)
                            dve.wait_ge(spread_done, i + 1)
                            if t >= 2:
                                dve.wait_ge(big_ready, i - 3)
                            dve.tensor_tensor(big[:, t % 2, qs, :].rearrange("p q (g t) -> p q g t", t=TG),
                                              ps_w[:, 2 * half:2 * half + 2, :]
                                              .rearrange("p a (q g t) -> p (a q) g t", g=GT, t=TG),
                                              hidden[:, qs, t * GT:(t + 1) * GT].unsqueeze(3)
                                              .broadcast_to([P, QC // 2, GT, TG]), ALU.mult
                                              ).then_inc(spread_ready, 1)
                        for half in range(2):
                            qs = slice(half * QC // 2, (half + 1) * QC // 2)
                            dve.wait_ge(big_high, 2 * t + half + 1)
                            dve.tensor_tensor(big_hl[:, t % 2, 1, qs, :], big[:, t % 2, qs, :],
                                              big_hl[:, t % 2, 0, qs, :].bitcast(F32), ALU.subtract
                                              ).then_inc(big_ready, 1)
                    if t >= 1:
                        u = t - 1
                        dve.wait_ge(out_done, u + 1)
                        dve.tensor_tensor(st.x[:, u, :], st.x[:, u, :], ps_o[:, u % 2, :], ALU.add
                                          ).then_inc(out_ready, 1)

            @block.tensor
            def _(pe):
                pe.wait_ge(loaded, 16)
                for t in range(TT):
                    turn_tile(pe, ps_t, st, t, xn_ready, xnT_ready, xnT_turned)
                for q in range(2):
                    pe.wait_ge(xnT_ready, (q + 1) * TT // 2)
                    for c in range(DC):
                        ins = pe.matmul(ps_l[:, q, :], ctl[:, c, :], st.xnT[:, c, q * 512:(q + 1) * 512],
                                        start=c == 0, stop=c == DC - 1)
                ins.then_inc(scored, 1)
                pe.wait_ge(mask_ready, 1)
                for t in range(TT):
                    ins = pe.transpose(ps_a[:, t * SE:(t + 1) * SE], maskT[:, t * P:(t + 1) * P],
                                       st.ident[0:SE, 0:SE])
                ins.then_inc(mask_turned, 1)
                for t in range(TT):
                    pe.wait_ge(block_ready, t + 1)
                    pe.wait_ge(low_ready, t + 1)
                    for c in range(DC):
                        u = t * DC + c
                        if u >= 2:
                            pe.wait_ge(taken_ready, u - 1)
                        else:
                            pe.wait_ge(xnT_ready, TT)
                        for part in range(2):
                            ins = pe.matmul(ps_t[:, u % 2, :], xn_hl[:, part, t, c * P:(c + 1) * P],
                                            block_mask[:, t % 2, :, :].rearrange("p g s -> p (g s)"),
                                            start=part == 0, stop=part == 1)
                        ins.then_inc(taken_done, 1)
                pe.wait_ge(f_in, 16)
                pe.wait_ge(taken_ready, TT * DC)
                for q in range(QC):
                    if q >= 2:
                        pe.wait_ge(hidden_ready, q - 1)
                    for j in range(4):
                        s = 4 * q + j
                        for c in range(DC):
                            ins = pe.matmul(ps_o[j * SF:(j + 1) * SF, q % 2, 0:NG],
                                            f1_sb[:, c, s * SF:(s + 1) * SF], takenT[:, c, :, s],
                                            start=c == 0, stop=c == DC - 1, tile_position=(0, j * SF))
                    ins.then_inc(hidden_done, 1)
                pe.wait_ge(mask_ready, 2)
                pe.wait_ge(consts, 1)
                def spread_tile(t):
                    for half in range(2):
                        if t >= 1:
                            pe.wait_ge(spread_ready, 2 * t + half - 1)
                        for j in range(QC // 2):
                            ins = pe.matmul(ps_w[:, 2 * half + j // 4, j % 4 * P:(j % 4 + 1) * P],
                                            spread[:, half * QC // 2 + j, :], maskT_16[:, t * P:(t + 1) * P],
                                            start=True, stop=True)
                        ins.then_inc(spread_done, 1)

                spread_tile(0)
                pe.wait_ge(f2_ready, QC // F2Q)
                pe.wait_ge(hidden_ready, QC)
                for t in range(TT):
                    if t + 1 < TT:
                        spread_tile(t + 1)
                    if t >= 2:
                        pe.wait_ge(out_ready, t - 1)
                    pe.wait_ge(big_ready, 2 * t + 2)
                    product(pe, ps_o[:, t % 2, :], lambda a, q: big_hl[:, t % 2, a, q, :],
                            lambda a, q: f2_hl[:, a, q, :], QC, True, True).then_inc(out_done, 1)

            @block.scalar
            def _(act):
                for t in range(TT):
                    take_tile(act, ps_t, st, t, xnT_ready, xnT_turned)
                for t in range(TT):
                    act.activation(xn_hl[:, 0, t, :], st.xn[:, t, :], ACT.Copy).then_inc(high_ready, 1)
                for t in range(TT):
                    for c in range(DC):
                        u = t * DC + c
                        act.wait_ge(taken_done, u + 1)
                        act.activation(takenT[:, c, t * GT:(t + 1) * GT, :],
                                       ps_t[:, u % 2, :].rearrange("p (g s) -> p g s", s=SE),
                                       ACT.Copy).then_inc(taken_ready, 1)
                for q in range(QC):
                    act.wait_ge(hidden_done, q + 1)
                    act.activation(hidden[:, q, :], ps_o[:, q % 2, 0:NG], ACT.Relu).then_inc(hidden_ready, 1)
                    if q % F2Q == 0:
                        i = q // F2Q
                        act.wait_ge(f2_in[i % 2], (i // 2 + 1) * 16)
                        act.activation(f2_hl[:, 0, q:q + F2Q, :], f2_raw[:, i % 2, :, :], ACT.Copy
                                       ).then_inc(f2_high, 1)
                for i in range(2 * TT):
                    t, half = i // 2, i % 2
                    qs = slice(half * QC // 2, (half + 1) * QC // 2)
                    act.wait_ge(spread_ready, i + 1)
                    if t >= 2:
                        act.wait_ge(out_done, t - 1)
                    act.activation(big_hl[:, t % 2, 0, qs, :], big[:, t % 2, qs, :], ACT.Copy).then_inc(big_high, 1)


def gnn_ffn_kernel(nc, x, src, dst, weights, out):
    with ExitStack() as ctx:
        kit = Kit(nc, ctx)
        with ExitStack() as graph_ctx:
            st = Persistent(kit, ctx, graph_ctx)
            stage_graph(kit, st, x, src, dst, *weights[0:2])
            stage_moe(kit, st, *weights[2:10])
            stage_sage(kit, st, *weights[10:15])
        stage_sets(kit, st, *weights[15:18], out)


_INS = ["x", "src", "dst", "L0_gnn_weight", "L0_gnn_bias", "L0_ffn_gate_w", "L0_ffn_gate_b", "L0_ffn_w1", "L0_ffn_b1",
        "L0_ffn_w2", "L0_ffn_b2", "L0_ffn_gamma", "L0_ffn_beta", "L1_gnn_gate_W", "L1_gnn_gate_b", "L1_gnn_Wl",
        "L1_gnn_bl", "L1_gnn_Wr", "L1_ffn_controller", "L1_ffn_f1", "L1_ffn_f2"]


def kernel(**inputs):
    import numpy as np
    import concourse.bacc as bacc
    from concourse.bass_utils import run_bass_kernel_spmd

    nc = bacc.Bacc("TRN2", target_bir_lowering=False, num_devices=1)
    arrays, args = {}, []
    for name in _INS:
        a = np.ascontiguousarray(inputs[name])
        arrays[f"in_{name}"] = a
        args.append(nc.dram_tensor(f"in_{name}", a.shape, mybir.dt.from_np(a.dtype), kind="ExternalInput").ap())
    out = nc.dram_tensor("out_0", (N, D), F32, kind="ExternalOutput").ap()
    gnn_ffn_kernel(nc, args[0], args[1], args[2], args[3:], out)
    results = run_bass_kernel_spmd(nc, [arrays], core_ids=[0])
    return results.results[0]["out_0"]
```
